# Optimizing a Trainium2 kernel written in Bass

```python
import numpy as np
import jax
import jax.numpy as jnp

def _softmax(x, axis=-1):
    return jax.nn.softmax(x, axis=axis)

def _gelu(x):
    return jax.nn.gelu(x, approximate=True)

def _silu(x):
    return jax.nn.silu(x)

def _sigmoid(x):
    return jax.nn.sigmoid(x)

def _layernorm(x, axis=-1, eps=1e-05):
    m = jnp.mean(x, axis=axis, keepdims=True)
    v = jnp.var(x, axis=axis, keepdims=True)
    return (x - m) / jnp.sqrt(v + eps)

def _scatter_add(tgt, idx, src, axis=0):
    return tgt.at[idx].add(src)

def _segment_sum(src, seg, n):
    return jax.ops.segment_sum(src, seg, n)
kernel_name = 'mk_macaron_d1_jaxref_r8_ae86dd'

def setup_inputs(seed: int=0):
    np.random.seed(seed)
    _w = jnp.asarray

    def _L0_attn_setup():
        import jax, jax.numpy as jnp
        import numpy as np
        H, DK, DV = (16, 128, 128)
        EPS = 1e-06

        def _causal_dw_conv(x, w):
            K = w.shape[0]
            T = x.shape[1]
            xp = jnp.pad(x, ((0, 0), (K - 1, 0), (0, 0)))
            out = w[0] * xp[:, 0:T, :]
            for i in range(1, K):
                out = out + w[i] * xp[:, i:i + T, :]
            return out

        def _rmsnorm(h, w):
            hf = h.astype(jnp.float32)
            var = jnp.mean(hf * hf, axis=-1, keepdims=True)
            return (hf * jax.lax.rsqrt(var + EPS)).astype(h.dtype) * w

        def _l2norm(x):
            return x * jax.lax.rsqrt(jnp.sum(x * x, axis=-1, keepdims=True) + EPS)
        key = jax.random.key(seed)
        ks = jax.random.split(key, 32)
        B, T, D = (1, 128, 256)
        LOW, I = (128, 1024)
        KD, VD = (H * DK, H * DV)
        s = 0.02
        f = jnp.float32
        return {'x': jax.random.normal(ks[0], (B, T, D), f), 'wq': jax.random.normal(ks[1], (D, KD), f) * s, 'wk': jax.random.normal(ks[2], (D, KD), f) * s, 'wv': jax.random.normal(ks[3], (D, VD), f) * s, 'conv_q': jax.random.normal(ks[4], (4, KD), f) * 0.2, 'conv_k': jax.random.normal(ks[5], (4, KD), f) * 0.2, 'conv_v': jax.random.normal(ks[6], (4, VD), f) * 0.2, 'wfa': jax.random.normal(ks[7], (D, LOW), f) * s, 'wfb': jax.random.normal(ks[8], (LOW, H), f) * s, 'wb': jax.random.normal(ks[9], (D, H), f) * s, 'wga': jax.random.normal(ks[10], (D, LOW), f) * s, 'wgb': jax.random.normal(ks[11], (LOW, VD), f) * s, 'a_log': jax.random.normal(ks[12], (H,), f) * 0.1, 'dt_bias': jnp.ones((H,), f), 'o_norm_w': jnp.ones((DV,), f), 'wo': jax.random.normal(ks[13], (VD, D), f) * s, 'ln1_w': jnp.ones((D,), f), 'ln2_w': jnp.ones((D,), f), 'w_gate': jax.random.normal(ks[14], (D, I), f) * s, 'w_up': jax.random.normal(ks[15], (D, I), f) * s, 'w_down': jax.random.normal(ks[16], (I, D), f) * s}
    _L0_attn_in = _L0_attn_setup()

    def _L0_ffn_setup():
        import jax, jax.numpy as jnp
        import numpy as np
        IN_F, OUT_F = (256, 256)
        N_EXPERTS, RANK, TOP_K = (8, 128, 2)
        key = jax.random.key(seed)
        k_x, k_r, k_a, k_b = jax.random.split(key, 4)
        hidden_states = jax.random.normal(k_x, (4, 512, IN_F), dtype=jnp.float32)
        router_w = jax.random.normal(k_r, (IN_F, N_EXPERTS), dtype=jnp.float32) * IN_F ** (-0.5)
        Wa = jax.random.normal(k_a, (N_EXPERTS, IN_F, RANK), dtype=jnp.float32) * IN_F ** (-0.5)
        Wb = jax.random.normal(k_b, (N_EXPERTS, RANK, OUT_F), dtype=jnp.float32) * RANK ** (-0.5)
        return {'hidden_states': hidden_states, 'router_w': router_w, 'Wa': Wa, 'Wb': Wb}
    _L0_ffn_in = _L0_ffn_setup()
    _d = {'L0_attn_x': _L0_attn_in['x'], 'L0_attn_wq': _L0_attn_in['wq'], 'L0_attn_wk': _L0_attn_in['wk'], 'L0_attn_wv': _L0_attn_in['wv'], 'L0_attn_conv_q': _L0_attn_in['conv_q'], 'L0_attn_conv_k': _L0_attn_in['conv_k'], 'L0_attn_conv_v': _L0_attn_in['conv_v'], 'L0_attn_wfa': _L0_attn_in['wfa'], 'L0_attn_wfb': _L0_attn_in['wfb'], 'L0_attn_wb': _L0_attn_in['wb'], 'L0_attn_wga': _L0_attn_in['wga'], 'L0_attn_wgb': _L0_attn_in['wgb'], 'L0_attn_a_log': _L0_attn_in['a_log'], 'L0_attn_dt_bias': _L0_attn_in['dt_bias'], 'L0_attn_o_norm_w': _L0_attn_in['o_norm_w'], 'L0_attn_wo': _L0_attn_in['wo'], 'L0_attn_ln1_w': _L0_attn_in['ln1_w'], 'L0_attn_ln2_w': _L0_attn_in['ln2_w'], 'L0_attn_w_gate': _L0_attn_in['w_gate'], 'L0_attn_w_up': _L0_attn_in['w_up'], 'L0_attn_w_down': _L0_attn_in['w_down'], 'L0_ffn_router_w': _L0_ffn_in['router_w'], 'L0_ffn_Wa': _L0_ffn_in['Wa'], 'L0_ffn_Wb': _L0_ffn_in['Wb']}
    _x0 = _d['L0_attn_x']
    _d['L0_attn_x'] = jax.random.normal(jax.random.fold_in(jax.random.key(seed), 1), (8, 256, 256), dtype=_x0.dtype)
    del _x0
    return _d

def reference(L0_attn_x, L0_attn_wq, L0_attn_wk, L0_attn_wv, L0_attn_conv_q, L0_attn_conv_k, L0_attn_conv_v, L0_attn_wfa, L0_attn_wfb, L0_attn_wb, L0_attn_wga, L0_attn_wgb, L0_attn_a_log, L0_attn_dt_bias, L0_attn_o_norm_w, L0_attn_wo, L0_attn_ln1_w, L0_attn_ln2_w, L0_attn_w_gate, L0_attn_w_up, L0_attn_w_down, L0_ffn_router_w, L0_ffn_Wa, L0_ffn_Wb):

    def _L0_attn_ref(x, wq, wk, wv, conv_q, conv_k, conv_v, wfa, wfb, wb, wga, wgb, a_log, dt_bias, o_norm_w, wo, ln1_w, ln2_w, w_gate, w_up, w_down):
        import jax, jax.numpy as jnp
        import numpy as np
        H, DK, DV = (16, 128, 128)
        EPS = 1e-06

        def _causal_dw_conv(x, w):
            K = w.shape[0]
            T = x.shape[1]
            xp = jnp.pad(x, ((0, 0), (K - 1, 0), (0, 0)))
            out = w[0] * xp[:, 0:T, :]
            for i in range(1, K):
                out = out + w[i] * xp[:, i:i + T, :]
            return out

        def _rmsnorm(h, w):
            hf = h.astype(jnp.float32)
            var = jnp.mean(hf * hf, axis=-1, keepdims=True)
            return (hf * jax.lax.rsqrt(var + EPS)).astype(h.dtype) * w

        def _l2norm(x):
            return x * jax.lax.rsqrt(jnp.sum(x * x, axis=-1, keepdims=True) + EPS)
        B, T, D = x.shape
        h = _rmsnorm(x, ln1_w)
        q = jax.nn.silu(_causal_dw_conv(h @ wq, conv_q)).reshape(B, T, H, DK)
        k = jax.nn.silu(_causal_dw_conv(h @ wk, conv_k)).reshape(B, T, H, DK)
        v = jax.nn.silu(_causal_dw_conv(h @ wv, conv_v)).reshape(B, T, H, DV)
        q = _l2norm(q) * DK ** (-0.5)
        k = _l2norm(k)
        g = -jnp.exp(a_log) * jax.nn.softplus(h @ wfa @ wfb + dt_bias)
        beta = jax.nn.sigmoid(h @ wb)

        def step(S, inp):
            qt, kt, vt, gt, bt = inp
            S = S * jnp.exp(gt)[..., None, None]
            kS = jnp.einsum('bhk,bhkv->bhv', kt, S)
            S = S + bt[..., None, None] * (kt[..., :, None] * (vt - kS)[..., None, :])
            ot = jnp.einsum('bhk,bhkv->bhv', qt, S)
            return (S, ot)
        S0 = jnp.zeros((B, H, DK, DV), x.dtype)
        xs = (q.transpose(1, 0, 2, 3), k.transpose(1, 0, 2, 3), v.transpose(1, 0, 2, 3), g.transpose(1, 0, 2), beta.transpose(1, 0, 2))
        _, o = jax.lax.scan(step, S0, xs)
        o = o.transpose(1, 0, 2, 3)
        gate = (h @ wga @ wgb).reshape(B, T, H, DV)
        o = _rmsnorm(o, o_norm_w) * jax.nn.silu(gate.astype(jnp.float32))
        o = o.astype(x.dtype).reshape(B, T, H * DV) @ wo
        x = x + o
        h2 = _rmsnorm(x, ln2_w)
        mlp = jax.nn.silu(h2 @ w_gate) * (h2 @ w_up) @ w_down
        return x + mlp

    def _L0_ffn_ref(hidden_states, router_w, Wa, Wb):
        import jax, jax.numpy as jnp
        import numpy as np
        IN_F, OUT_F = (256, 256)
        N_EXPERTS, RANK, TOP_K = (8, 128, 2)
        B, S, D = hidden_states.shape
        x = hidden_states.reshape(-1, D)
        norm = jnp.maximum(jnp.linalg.norm(x, axis=-1, keepdims=True), 1e-12)
        router_logits = x / norm @ router_w
        routing_weights = jax.nn.softmax(router_logits.astype(jnp.float32), axis=-1)
        rw, selected_experts = jax.lax.top_k(routing_weights, TOP_K)
        rw = rw / jnp.sum(rw, axis=-1, keepdims=True)
        rw = rw.astype(hidden_states.dtype)
        combine = jnp.sum(jax.nn.one_hot(selected_experts, N_EXPERTS, dtype=rw.dtype) * rw[..., None], axis=1)
        out = jnp.zeros((x.shape[0], OUT_F), dtype=hidden_states.dtype)
        for e in range(N_EXPERTS):
            out = out + combine[:, e, None] * (x @ Wa[e] @ Wb[e])
        return out.reshape(B, S, OUT_F)
    x = L0_attn_x
    x = x + 0.5 * _L0_ffn_ref(_layernorm(x, axis=-1), L0_ffn_router_w, L0_ffn_Wa, L0_ffn_Wb)
    x = x + _L0_attn_ref(_layernorm(x, axis=-1), L0_attn_wq, L0_attn_wk, L0_attn_wv, L0_attn_conv_q, L0_attn_conv_k, L0_attn_conv_v, L0_attn_wfa, L0_attn_wfb, L0_attn_wb, L0_attn_wga, L0_attn_wgb, L0_attn_a_log, L0_attn_dt_bias, L0_attn_o_norm_w, L0_attn_wo, L0_attn_ln1_w, L0_attn_ln2_w, L0_attn_w_gate, L0_attn_w_up, L0_attn_w_down)
    x = x + 0.5 * _L0_ffn_ref(_layernorm(x, axis=-1), L0_ffn_router_w, L0_ffn_Wa, L0_ffn_Wb)
    return x

_drawn_inputs = setup_inputs


def setup_inputs(seed=0):
    import zlib

    import numpy as np

    out = dict(_drawn_inputs(seed))
    spreads = {'L0_attn_dt_bias': (1.0, 0.6),
     'L0_attn_o_norm_w': (1.0, 0.6),
     'L0_attn_ln1_w': (1.0, 0.6),
     'L0_attn_ln2_w': (1.0, 0.6)}
    factors = {'L0_attn_wq': 5.266,
     'L0_attn_wk': 5.579,
     'L0_attn_wv': 4.944,
     'L0_attn_conv_q': 5.317,
     'L0_attn_conv_k': 5.561,
     'L0_attn_conv_v': 5.129,
     'L0_attn_wfa': 8.0,
     'L0_attn_wfb': 8.0,
     'L0_attn_wb': 8.0,
     'L0_attn_wga': 5.665,
     'L0_attn_wgb': 5.591,
     'L0_attn_a_log': 8.0,
     'L0_attn_wo': 5.23,
     'L0_attn_w_gate': 8.0,
     'L0_attn_w_up': 8.0,
     'L0_attn_w_down': 8.0}
    for name, (base, spread) in spreads.items():
        noise = np.random.default_rng([zlib.crc32(name.encode()), seed]).standard_normal(out[name].shape)
        drawn = base * np.exp(spread * noise) if base else spread * noise
        out[name] = jnp.asarray(drawn.astype(out[name].dtype))
    for name, factor in factors.items():
        out[name] = (out[name] * factor).astype(out[name].dtype)
    return out
```

```python
from contextlib import ExitStack

import concourse.bass as bass
from concourse import mybir

F32 = mybir.dt.float32
F32R = mybir.dt.float32r
U32 = mybir.dt.uint32
ALU = mybir.AluOpType
ACT = mybir.ActivationFunctionType
AX = mybir.AxisListType
LOG_EXP = "natural_log_exp_and_others"
SILU = "silu_and_others"
SILU_SET = "silu_and_others"

P = 128
B, T, D = 8, 256, 256
KT = D // P
H, DH = 16, 128
TAPS = 4
NE, RANK = 8, 128
LOW, INNER = 128, 1024
TILES = B * T // P
STEP = 4
STEPS = TILES // STEP
N = STEP * P
SUB = 32
SUBS = P // SUB
EPS = 1e-6
LN_EPS = 1e-5
FAR = -30720.0
G_HI, G_LO, BETA, CONV, TABLE = 0, TILES, 2 * TILES, 3 * TILES, 3 * TILES + 3 * TAPS


def wait(eng, sem, value):
    if isinstance(value, int) and value <= 0:
        return
    eng.wait_ge(sem, value)


def spread(ap, shape, axis=2):
    return ap.unsqueeze(axis).to_broadcast(shape)


class Semaphores:

    def __init__(self, nc, ctx, prefix):
        self.nc, self.prefix, self.all = nc, prefix, {}
        ctx.callback(self.release)

    def __call__(self, name):
        if name not in self.all:
            self.all[name] = self.nc.alloc_semaphore(name=self.prefix + name)
        return self.all[name]

    def release(self):
        self.nc.clear_and_free_semaphores(list(self.all.values()))
        self.nc.all_engine_barrier()



def ffn_buffers(nc, ctx, pre):
    def sb(name, shape, dt=F32):
        return ctx.enter_context(nc.sbuf_tensor(pre + name, shape, dt))

    class Buf:
        pass

    b = Buf()
    b.wa_raw = sb("wa_raw", [P, KT, NE * RANK])
    b.wa_hi = sb("wa_hi", [P, KT, NE * RANK], F32R)
    b.wa_lo = sb("wa_lo", [P, KT, NE * RANK], F32R)
    b.wb = sb("wb", [RANK, NE, D])
    b.router = sb("router", [P, KT, NE])
    b.sel_raw = sb("sel_raw", [2 * NE, NE, P])
    b.sel = sb("sel", [2 * NE, NE, P], F32R)
    b.iota = sb("iota", [P, NE])
    b.stats = sb("stats", [P, STEP, 6])
    b.mv = sb("mv", [P, STEP, 2])
    b.fence = sb("fence", [P, 2])
    b.lnv = sb("lnv", [P, STEP])
    b.rstd = sb("rstd", [P, STEP])
    b.q1 = sb("q1", [P, STEP])
    b.q2 = sb("q2", [P, STEP])
    b.q3 = sb("q3", [P, STEP])
    b.lnq = sb("lnq", [P, STEP])
    b.rn = sb("rn", [P, STEP])
    b.xn = sb("xn", [P, STEP, D])
    b.xnT = sb("xnT", [P, KT, N])
    b.xnT_hi = sb("xnT_hi", [P, KT, N], F32R)
    b.xnT_lo = sb("xnT_lo", [P, KT, N], F32R)
    b.logits = sb("logits", [P, STEP, NE])
    b.top = sb("top", [P, STEP, 8])
    b.topi = sb("topi", [P, STEP, 8], U32)
    b.topf = sb("topf", [P, STEP, 8])
    b.diff = sb("diff", [P, STEP, NE])
    b.diff2 = sb("diff2", [P, STEP, NE])
    b.ex = sb("ex", [P, STEP, NE])
    b.hit0 = sb("hit0", [P, STEP, NE])
    b.hit1 = sb("hit1", [P, STEP, NE])
    b.hits = sb("hits", [P, STEP, NE])
    b.chosen = sb("chosen", [P, STEP, NE])
    b.total = sb("total", [P, STEP])
    b.rtotal = sb("rtotal", [P, STEP])
    b.comb = sb("comb", [P, STEP, NE])
    b.comb2 = sb("comb2", [P, STEP, 2 * NE], F32R)
    b.combT = sb("combT", [2 * NE, N], F32R)
    b.wide = [sb(f"wide{i}", [P, N]) for i in range(2)]
    b.hc = [sb(f"hc{i}", [P, N]) for i in range(2)]
    return b


def ffn_load(sp, b, S, router_w, Wa, Wb):
    sp.dma_start(b.wa_raw[:].rearrange("p k (e r) -> p k e r", e=NE)[:, 0],
                 Wa[:, 0:P, :].rearrange("e p r -> p e r")).then_inc(S("w_in"), 16)
    sp.dma_start(b.wa_raw[:].rearrange("p k (e r) -> p k e r", e=NE)[:, 1],
                 Wa[:, P:D, :].rearrange("e p r -> p e r")).then_inc(S("w_in"), 16)
    sp.dma_start(b.wb[:], Wb.rearrange("e r d -> r e d")).then_inc(S("wb_in"), 16)
    sp.dma_start(b.router[:], router_w.rearrange("(k p) e -> p k e", p=P)).then_inc(S("router_in"), 16)


def ffn_constants_pool(nc, pool, b, S):
    nc.gpsimd.memset(b.sel_raw[:], 0.0).then_inc(S("sel_made"), 1)
    pool.wait_ge(S("sel_made"), 1)
    for part in range(2):
        nc.gpsimd.affine_select(out=b.sel_raw[:], in_=b.sel_raw[:], compare_op=ALU.not_equal, fill=1.0,
                                base=-NE * part, pattern=[[-1, NE], [0, P]],
                                channel_multiplier=1).then_inc(S("sel_made"), 1)
        pool.wait_ge(S("sel_made"), 2 + part)
    nc.gpsimd.iota(b.iota[:], pattern=[[1, NE]], base=0, channel_multiplier=0,
                   allow_small_or_imprecise_dtypes=True).then_inc(S("iota_made"), 1)


def ffn_constants_vector(nc, dve, b, S):
    dve.wait_ge(S("sel_made"), 3)
    nc.vector.tensor_copy(b.sel[:], b.sel_raw[:]).then_inc(S("w_hi"), 1)
    dve.wait_ge(S("w_in"), 32)
    nc.vector.tensor_copy(b.wa_hi[:], b.wa_raw[:]).then_inc(S("w_hi"), 1)
    dve.wait_ge(S("w_hi"), 2)
    nc.vector.tensor_tensor(b.wa_lo[:], b.wa_raw[:], b.wa_hi[:].bitcast(F32),
                            ALU.subtract).then_inc(S("w_split"), 1)
    dve.wait_ge(S("iota_made"), 1)


def norm_stats_vector(nc, dve, b, S, n, src, tag):
    for t in range(STEP):
        last = nc.vector.bn_stats(b.stats[:, t, :], src[:, t, :])
    last.then_inc(S(tag + "stats"), 1)
    dve.wait_ge(S(tag + "stats"), n + 1)
    nc.vector.memset(b.fence[:, 0:1], 0.0)
    for t in range(STEP):
        last = nc.vector.bn_aggr(b.mv[:, t, :], b.stats[:, t, :])
    last.then_inc(S(tag + "mv"), 1)


def ffn_vector_front(nc, dve, b, S, n, x, bank_c, wait_x):
    wait_x(dve)
    norm_stats_vector(nc, dve, b, S, n, x, "f_")
    dve.wait_ge(S("rstd"), n + 1)
    for t in range(STEP):
        last = nc.vector.tensor_scalar(b.xn[:, t, :], x[:, t, :], b.mv[:, t, 0:1], b.rstd[:, t:t + 1],
                                       ALU.subtract, ALU.mult)
    last.then_inc(S("xn"), 1)
    nc.vector.tensor_tensor(b.q1[:], b.mv[:, :, 1], b.rstd[:], ALU.mult).then_inc(S("q1"), 1)
    dve.wait_ge(S("q1"), n + 1)
    nc.vector.tensor_tensor(b.q2[:], b.q1[:], b.rstd[:], ALU.mult).then_inc(S("q2"), 1)
    dve.wait_ge(S("q2"), n + 1)
    nc.vector.tensor_scalar(b.q3[:], b.q2[:], float(D), 1e-24, ALU.mult, ALU.max).then_inc(S("q3"), 1)
    dve.wait_ge(S("xnT"), n + 1)
    nc.vector.tensor_copy(b.xnT_hi[:], b.xnT[:]).then_inc(S("xnT_hi"), 1)
    dve.wait_ge(S("xnT_hi"), n + 1)
    nc.vector.tensor_tensor(b.xnT_lo[:], b.xnT[:], b.xnT_hi[:].bitcast(F32), ALU.subtract).then_inc(S("xnT_lo"), 1)
    dve.wait_ge(S("router"), n + 1)
    nc.vector.tensor_copy(b.logits[:], bank_c[:, 0:STEP * NE].rearrange("p (t e) -> p t e", t=STEP)
                          ).then_inc(S("logits"), 1)
    dve.wait_ge(S("logits"), n + 1)
    nc.vector.memset(b.fence[:, 1:2], 0.0)
    for t in range(STEP):
        last = nc.vector.max(b.top[:, t, :], b.logits[:, t, :])
    last.then_inc(S("top"), 1)
    dve.wait_ge(S("top"), n + 1)
    nc.vector.tensor_tensor(b.diff[:], b.logits[:], b.top[:, :, 0:1].to_broadcast([P, STEP, NE]),
                            ALU.subtract).then_inc(S("diff"), 1)
    for t in range(STEP):
        last = nc.vector.max_index(b.topi[:, t, :], b.top[:, t, :], b.logits[:, t, :])
    last.then_inc(S("topi"), 1)
    dve.wait_ge(S("diff"), n + 1)
    dve.wait_ge(S("rn"), n + 1)
    nc.vector.tensor_tensor(b.diff2[:], b.diff[:], spread(b.rn[:, :], [P, STEP, NE]),
                            ALU.mult).then_inc(S("diff2"), 1)
    dve.wait_ge(S("topi"), n + 1)
    nc.vector.tensor_copy(b.topf[:], b.topi[:]).then_inc(S("topf"), 1)
    dve.wait_ge(S("topf"), n + 1)
    names = spread(b.iota[:, :], [P, STEP, NE], 1)
    nc.vector.tensor_tensor(b.hit0[:], names, b.topf[:, :, 0:1].to_broadcast([P, STEP, NE]), ALU.is_equal)
    nc.vector.tensor_tensor(b.hit1[:], names, b.topf[:, :, 1:2].to_broadcast([P, STEP, NE]),
                            ALU.is_equal).then_inc(S("hit"), 1)
    dve.wait_ge(S("hit"), n + 1)
    nc.vector.tensor_tensor(b.hits[:], b.hit0[:], b.hit1[:], ALU.add).then_inc(S("hits"), 1)
    dve.wait_ge(S("hits"), n + 1)
    dve.wait_ge(S("ex"), n + 1)
    nc.vector.tensor_tensor(b.chosen[:], b.ex[:], b.hits[:], ALU.mult).then_inc(S("chosen"), 1)
    dve.wait_ge(S("chosen"), n + 1)
    nc.vector.tensor_reduce(b.total[:], b.chosen[:], AX.X, ALU.add).then_inc(S("total"), 1)
    dve.wait_ge(S("total"), n + 1)
    nc.vector.reciprocal(b.rtotal[:], b.total[:]).then_inc(S("rtotal"), 1)
    dve.wait_ge(S("rtotal"), n + 1)
    nc.vector.scalar_tensor_tensor(out=b.comb[:], in0=b.chosen[:], scalar=0.5,
                                   in1=spread(b.rtotal[:, :], [P, STEP, NE]),
                                   op0=ALU.mult, op1=ALU.mult).then_inc(S("comb"), 1)
    dve.wait_ge(S("comb"), n + 1)
    nc.vector.tensor_copy(b.comb2[:, :, 0:NE], b.comb[:]).then_inc(S("comb_hi"), 1)
    dve.wait_ge(S("comb_hi"), n + 1)
    nc.vector.tensor_tensor(b.comb2[:, :, NE:], b.comb[:], b.comb2[:, :, 0:NE].bitcast(F32),
                            ALU.subtract).then_inc(S("comb2"), 1)


def ffn_vector_experts(nc, dve, b, S, n, bank_h):
    for e in range(NE):
        dve.wait_ge(S("wide"), n * NE + e + 1)
        if e >= 2:
            dve.wait_ge(S("down"), n * NE + e - 1)
        nc.vector.tensor_tensor(b.hc[e % 2][:], bank_h[e % 2][:], b.wide[e % 2][:],
                                ALU.mult).then_inc(S("hc"), 1)


def ffn_scalar(nc, act, b, S, n, bank_t, bank_c):
    nc.scalar.preload_act_table_set(LOG_EXP)
    act.wait_ge(S("f_mv"), n + 1)
    nc.scalar.activation(b.lnv[:], b.mv[:, :, 1], ACT.Ln, bias=LN_EPS).then_inc(S("lnv"), 1)
    act.wait_ge(S("lnv"), n + 1)
    nc.scalar.activation(b.rstd[:], b.lnv[:], ACT.Exp, scale=-0.5).then_inc(S("rstd"), 1)
    act.wait_ge(S("xT"), n + 1)
    for k in range(KT):
        last = nc.scalar.activation(b.xnT[:, k, :], bank_t[k][:], ACT.Copy)
    last.then_inc(S("xnT"), 1)
    act.wait_ge(S("q3"), n + 1)
    nc.scalar.activation(b.lnq[:], b.q3[:], ACT.Ln, scale=float(2 ** 40)).then_inc(S("lnq"), 1)
    act.wait_ge(S("lnq"), n + 1)
    nc.scalar.activation(b.rn[:], b.lnq[:], ACT.Exp, scale=-0.5, bias=13.862943611198906).then_inc(S("rn"), 1)
    act.wait_ge(S("diff2"), n + 1)
    nc.scalar.activation(b.ex[:], b.diff2[:], ACT.Exp).then_inc(S("ex"), 1)
    act.wait_ge(S("cT"), n + 1)
    nc.scalar.activation(b.combT[:], bank_c[1][0:2 * NE, :], ACT.Copy).then_inc(S("combT"), 1)
    for e in range(NE):
        act.wait_ge(S("up"), n * NE + e + 1)
        if e >= 2:
            act.wait_ge(S("hc"), n * NE + e - 1)
        nc.scalar.activation(b.wide[e % 2][:], bank_c[e % 2][:], ACT.Copy).then_inc(S("wide"), 1)


def ffn_tensor(nc, pe, b, S, n, ident, bank_t, bank_c, bank_h, bank_o, wait_o):
    pe.wait_ge(S("xn"), n + 1)
    for k in range(KT):
        for t in range(STEP):
            last = nc.tensor.transpose(bank_t[k][:, t * P:(t + 1) * P], b.xn[:, t, k * P:(k + 1) * P], ident[:])
    last.then_inc(S("xT"), 1)
    pe.wait_ge(S("xnT"), n + 1)
    for t in range(STEP):
        for k in range(KT):
            last = nc.tensor.matmul(bank_c[0][:, t * NE:(t + 1) * NE], b.xnT[:, k, t * P:(t + 1) * P],
                                    b.router[:, k, :], start=(k == 0), stop=(k == KT - 1))
    last.then_inc(S("router"), 1)
    pe.wait_ge(S("comb2"), n + 1)
    for t in range(STEP):
        last = nc.tensor.transpose(bank_c[1][0:2 * NE, t * P:(t + 1) * P], b.comb2[:, t, :].bitcast(F32), ident[:])
    last.then_inc(S("cT"), 1)

    def up(e):
        cols = slice(e * RANK, (e + 1) * RANK)
        parts = [(w, x, k) for w, x in ((b.wa_hi, b.xnT_hi), (b.wa_hi, b.xnT_lo), (b.wa_lo, b.xnT_hi))
                 for k in range(KT)]
        for i, (w, x, k) in enumerate(parts):
            nc.tensor.matmul(bank_h[e % 2][:], w[:, k, cols], x[:, k, :], start=(i == 0), stop=(i == len(parts) - 1))
        if e == 0:
            pe.wait_ge(S("combT"), n + 1)
        nc.tensor.matmul(bank_c[e % 2][:], b.sel[:, e, :], b.combT[:], start=True,
                         stop=True).then_inc(S("up"), 1)

    pe.wait_ge(S("xnT_lo"), n + 1)
    up(0)
    up(1)
    wait_o(pe)
    for e in range(NE):
        pe.wait_ge(S("hc"), n * NE + e + 1)
        for t in range(STEP):
            last = nc.tensor.matmul(bank_o[t // 2][:, (t % 2) * D:(t % 2 + 1) * D], b.hc[e % 2][:, t * P:(t + 1) * P],
                                    b.wb[:, e, :], start=(e == 0 and t % 2 == 0), stop=(e == NE - 1),
                                    skip_group_check=True)
        last.then_inc(S("down"), 1)
        if e + 2 < NE:
            up(e + 2)



def persistent_buffers(nc, ctx):
    def sb(name, shape, dt=F32):
        return ctx.enter_context(nc.sbuf_tensor(name, shape, dt))

    class Buf:
        pass

    g = Buf()
    g.ident = sb("ident", [P, P])
    g.ident_r = sb("ident_r", [P, P], F32R)
    g.upto = sb("upto", [P, P])
    g.after_r = sb("after_r", [P, P], F32R)
    g.far_r = sb("far_r", [P, P], F32R)
    g.ones = sb("ones", [P, 1])
    g.ln1 = sb("ln1", [P, KT])
    g.ln2 = sb("ln2", [P, KT])
    g.onorm = sb("onorm", [P, 1])
    g.acc = sb("acc", [P, TILES, D])
    return g


def attention_buffers(nc, ctx, g):
    def sb(name, shape, dt=F32):
        return ctx.enter_context(nc.sbuf_tensor(name, shape, dt))

    g.hT_hi = sb("hT_hi", [P, KT, TILES * P], F32R)
    g.hT_lo = sb("hT_lo", [P, KT, TILES * P], F32R)
    g.gateT = sb("gateT", [LOW, TILES * P])
    g.table = sb("table", [P, H, TABLE])
    g.eg = sb("eg", [P, H, TILES])
    g.neg_eg = sb("neg_eg", [P, H, TILES])



def stage_one(nc, g, d):
    with ExitStack() as ctx:
        def sb(name, shape, dt=F32):
            return ctx.enter_context(nc.sbuf_tensor("s1_" + name, shape, dt))

        S = Semaphores(nc, ctx, "s1_")
        b = ffn_buffers(nc, ctx, "s1_")
        x_in = sb("x_in", [P, STEP, D])
        x1 = sb("x1", [P, STEP, D])
        hid = sb("hid", [P, STEP, D])
        hT = sb("hT", [P, KT, N])
        fa = sb("fa", [LOW, N])
        wfa = sb("wfa", [P, KT, LOW])
        wga = sb("wga", [P, KT, LOW])
        wfb = sb("wfb", [LOW, H])
        wbeta = sb("wbeta", [P, KT, H])
        a_log = sb("a_log", [P, H])
        ea = sb("ea", [P, H])
        dtb = sb("dtb", [P, H])
        mask = sb("mask", [P, 3, P])
        conv_rows = sb("conv_rows", [TAPS * H, 3, P])
        lnv2 = sb("lnv2", [P, STEP])
        rstd2 = sb("rstd2", [P, STEP])
        v1 = sb("v1", [P, STEP])
        v2 = sb("v2", [P, STEP])
        lnr = sb("lnr", [P, STEP])
        rms = sb("rms", [P, STEP])
        both = sb("both", [P, STEP])
        z = sb("z", [P, STEP, H])
        zb = sb("zb", [P, STEP, H])
        az = sb("az", [P, STEP, H])
        ez = sb("ez", [P, STEP, H])
        lz = sb("lz", [P, STEP, H])
        ezb = sb("ezb", [P, STEP, H])
        sp_ = sb("softplus", [P, STEP, H])
        decay = sb("decay", [P, STEP, H])
        decay_hi = sb("decay_hi", [P, STEP, H], F32R)
        ezb1 = sb("ezb1", [P, STEP, H])
        beta = sb("beta", [P, STEP, H])

        bank = [ctx.enter_context(nc.psum_tensor(f"s1_bank{i}", [P, N], F32)) for i in range(8)]
        bank_t, bank_c, bank_h, bank_o = bank[0:2], bank[2:4], bank[4:6], bank[6:8]
        x_tiles = d.x.rearrange("b (c p) d -> p (b c) d", p=P)
        x1_tiles = d.x1_dram.rearrange("(n p) d -> p n d", p=P)
        table_t = g.table[:].rearrange("p h f -> p f h")
        block = ctx.enter_context(nc.Block())

        @block.sync
        def _(sp):
            sp.dma_start(x_in[:], x_tiles[:, 0:STEP, :]).then_inc(S("moved"), 16)
            ffn_load(sp, b, S, d.router_w, d.Wa, d.Wb)
            for dst, src in ((wfa, d.wfa), (wga, d.wga), (wbeta, d.wb)):
                sp.dma_start(dst[:], src.rearrange("(k p) n -> p k n", p=P)).then_inc(S("gates_in"), 16)
            sp.dma_start(wfb[:], d.wfb).then_inc(S("gates_in"), 16)
            for dst, src in ((a_log, d.a_log), (dtb, d.dt_bias)):
                sp.dma_start(dst[:], src.rearrange("(a h) -> a h", a=1).to_broadcast([P, H])).then_inc(S("gates_in"), 16)
            for dst, src in ((g.ln1, d.ln1_w), (g.ln2, d.ln2_w)):
                for k in range(KT):
                    sp.dma_start(dst[:, k:k + 1], src[k * P:(k + 1) * P].rearrange("(p a) -> p a", a=1)
                                 ).then_inc(S("gates_in"), 16)
            sp.dma_start(g.onorm[:], d.o_norm_w.rearrange("(p a) -> p a", a=1)).then_inc(S("gates_in"), 16)
            for c, src in enumerate((d.conv_q, d.conv_k, d.conv_v)):
                sp.dma_start(conv_rows[:, c, :], src.rearrange("t (h p) -> (t h) p", p=P)).then_inc(S("conv_in"), 16)
            with sp.Fori(0, STEPS - 1) as n:
                sp.wait_ge(S("x1"), n + 1)
                sp.dma_start(x_in[:], x_tiles[:, bass.ds(n * STEP + STEP, STEP), :]).then_inc(S("moved"), 16)
                sp.dma_start(x1_tiles[:, bass.ds(n * STEP, STEP), :], x1[:]).then_inc(S("moved"), 16)
            sp.wait_ge(S("x1"), STEPS)
            sp.dma_start(x1_tiles[:, TILES - STEP:TILES, :], x1[:]).then_inc(S("moved"), 16)
            sp.wait_ge(S("moved"), 32 * STEPS)

        @block.gpsimd
        def _(pool):
            nc.gpsimd.memset(g.ones[:], 1.0).then_inc(S("ones"), 1)
            nc.gpsimd.memset(g.ident[:], 0.0).then_inc(S("blank"), 1)
            nc.gpsimd.memset(g.upto[:], 1.0).then_inc(S("blank"), 1)
            nc.gpsimd.memset(mask[:, 0, :], 1.0).then_inc(S("blank"), 1)
            nc.gpsimd.memset(mask[:, 1, :], 0.0).then_inc(S("blank"), 1)
            pool.wait_ge(S("blank"), 4)
            nc.gpsimd.affine_select(out=g.ident[:], in_=g.ident[:], compare_op=ALU.not_equal, fill=1.0, base=0,
                                    pattern=[[-1, P]], channel_multiplier=1).then_inc(S("masks"), 1)
            nc.gpsimd.affine_select(out=g.upto[:], in_=g.upto[:], compare_op=ALU.is_ge, fill=0.0, base=0,
                                    pattern=[[1, P]], channel_multiplier=-1).then_inc(S("masks"), 1)
            nc.gpsimd.affine_select(out=mask[:, 0, :], in_=mask[:, 0, :], compare_op=ALU.is_ge, fill=0.0, base=-1,
                                    pattern=[[-1, P]], channel_multiplier=1).then_inc(S("masks"), 1)
            nc.gpsimd.affine_select(out=mask[:, 1, :], in_=mask[:, 1, :], compare_op=ALU.is_ge, fill=FAR, base=0,
                                    pattern=[[1, P]], channel_multiplier=-1).then_inc(S("masks"), 1)
            ffn_constants_pool(nc, pool, b, S)

        @block.vector
        def _(dve):
            dve.wait_ge(S("masks"), 4)
            nc.vector.tensor_copy(g.after_r[:], mask[:, 0, :])
            nc.vector.tensor_copy(g.far_r[:], mask[:, 1, :])
            nc.vector.tensor_copy(g.ident_r[:], g.ident[:]).then_inc(S("masks_r"), 1)
            ffn_constants_vector(nc, dve, b, S)
            dve.wait_ge(S("conv_T"), 1)
            for c in range(3):
                last = nc.vector.tensor_copy(
                    table_t[:, CONV + TAPS * c:CONV + TAPS * (c + 1), :],
                    bank[0][:, c * TAPS * H:(c + 1) * TAPS * H].rearrange("p (t h) -> p t h", t=TAPS))
            last.then_inc(S("conv"), 1)
            dve.wait_ge(S("conv"), 1)
            dve.wait_ge(S("gates_in"), 16 * 11)
            dve.wait_ge(S("ea"), 1)
            with dve.Fori(0, STEPS) as n:
                ffn_vector_front(nc, dve, b, S, n, x_in, bank_c[0],
                                 lambda e: e.wait_ge(S("moved"), n * 32 + 16))
                ffn_vector_experts(nc, dve, b, S, n, bank_h)
                dve.wait_ge(S("down"), n * NE + NE)
                for i in range(2):
                    last = nc.vector.tensor_tensor(
                        x1[:, 2 * i:2 * i + 2, :], bank_o[i][:].rearrange("p (t d) -> p t d", t=2),
                        x_in[:, 2 * i:2 * i + 2, :], ALU.add)
                last.then_inc(S("x1"), 1)
                dve.wait_ge(S("x1"), n + 1)
                norm_stats_vector(nc, dve, b, S, n, x1, "a_")
                dve.wait_ge(S("rstd2"), n + 1)
                nc.vector.tensor_tensor(v1[:], b.mv[:, :, 1], rstd2[:], ALU.mult).then_inc(S("v1"), 1)
                for t in range(STEP):
                    nc.vector.tensor_scalar(g.acc[:, bass.ds(n * STEP + t, 1), :], x1[:, t:t + 1, :], b.mv[:, t, 0:1],
                                            rstd2[:, t:t + 1], ALU.subtract, ALU.mult)
                dve.wait_ge(S("v1"), n + 1)
                nc.vector.tensor_tensor(v2[:], v1[:], rstd2[:], ALU.mult).then_inc(S("v2"), 1)
                dve.wait_ge(S("rms"), n + 1)
                nc.vector.tensor_tensor(both[:], rstd2[:], rms[:], ALU.mult).then_inc(S("both"), 1)
                dve.wait_ge(S("both"), n + 1)
                for t in range(STEP):
                    last = nc.vector.tensor_scalar(hid[:, t, :], x1[:, t, :], b.mv[:, t, 0:1], both[:, t:t + 1],
                                                   ALU.subtract, ALU.mult)
                last.then_inc(S("hid"), 1)
                dve.wait_ge(S("hT"), n + 1)
                nc.vector.tensor_scalar(g.hT_hi[:, :, bass.ds(n * N, N)], hT[:], 1.0, None, ALU.mult
                                        ).then_inc(S("hT_hi"), 1)
                dve.wait_ge(S("hT_hi"), n + 1)
                nc.vector.tensor_tensor(g.hT_lo[:, :, bass.ds(n * N, N)], hT[:],
                                        g.hT_hi[:, :, bass.ds(n * N, N)].bitcast(F32), ALU.subtract)
                dve.wait_ge(S("low"), n + 1)
                nc.vector.tensor_scalar(g.gateT[:, bass.ds(n * N, N)], bank_h[1][:], 1.0, None, ALU.mult)
                dve.wait_ge(S("gates"), n + 1)
                nc.vector.tensor_tensor(z[:], bank_c[0][:, 0:STEP * H].rearrange("p (t h) -> p t h", t=STEP),
                                        spread(dtb[:, :], [P, STEP, H], 1), ALU.add).then_inc(S("z"), 1)
                nc.vector.tensor_scalar(zb[:], bank_c[0][:, STEP * H:2 * STEP * H].rearrange("p (t h) -> p t h", t=STEP),
                                        -1.0, 80.0, ALU.mult, ALU.min).then_inc(S("zb"), 1)
                dve.wait_ge(S("lz"), n + 1)
                nc.vector.scalar_tensor_tensor(out=sp_[:], in0=z[:], scalar=0.0, in1=lz[:], op0=ALU.max,
                                               op1=ALU.add).then_inc(S("softplus"), 1)
                dve.wait_ge(S("softplus"), n + 1)
                nc.vector.scalar_tensor_tensor(out=decay[:], in0=sp_[:], scalar=-1.0,
                                               in1=spread(ea[:, :], [P, STEP, H], 1), op0=ALU.mult,
                                               op1=ALU.mult).then_inc(S("decay"), 1)
                dve.wait_ge(S("decay"), n + 1)
                nc.vector.tensor_copy(decay_hi[:], decay[:]).then_inc(S("decay_hi"), 1)
                dve.wait_ge(S("decay_hi"), n + 1)
                nc.vector.tensor_scalar(table_t[:, bass.ds(n * STEP, STEP), :], decay_hi[:].bitcast(F32), 1.0, None,
                                        ALU.mult)
                nc.vector.tensor_tensor(table_t[:, bass.ds(n * STEP + G_LO, STEP), :], decay[:],
                                        decay_hi[:].bitcast(F32), ALU.subtract)
                dve.wait_ge(S("ezb"), n + 1)
                nc.vector.tensor_scalar(ezb1[:], ezb[:], 1.0, None, ALU.add).then_inc(S("ezb1"), 1)
                dve.wait_ge(S("ezb1"), n + 1)
                nc.vector.reciprocal(beta[:], ezb1[:]).then_inc(S("beta"), 1)
                dve.wait_ge(S("beta"), n + 1)
                nc.vector.tensor_scalar(table_t[:, bass.ds(n * STEP + BETA, STEP), :], beta[:], 1.0, None,
                                        ALU.mult).then_inc(S("table"), 1)
            dve.wait_ge(S("eg"), 1)
            nc.vector.tensor_scalar(g.neg_eg[:], g.eg[:], -1.0, None, ALU.mult)

        @block.scalar
        def _(act):
            nc.scalar.preload_act_table_set(LOG_EXP)
            act.wait_ge(S("gates_in"), 16 * 11)
            nc.scalar.activation(ea[:], a_log[:], ACT.Exp).then_inc(S("ea"), 1)
            with act.Fori(0, STEPS) as n:
                ffn_scalar(nc, act, b, S, n, bank_t, bank_c)
                act.wait_ge(S("a_mv"), n + 1)
                nc.scalar.activation(lnv2[:], b.mv[:, :, 1], ACT.Ln, bias=LN_EPS).then_inc(S("lnv2"), 1)
                act.wait_ge(S("lnv2"), n + 1)
                nc.scalar.activation(rstd2[:], lnv2[:], ACT.Exp, scale=-0.5).then_inc(S("rstd2"), 1)
                act.wait_ge(S("v2"), n + 1)
                nc.scalar.activation(lnr[:], v2[:], ACT.Ln, bias=EPS).then_inc(S("lnr"), 1)
                act.wait_ge(S("lnr"), n + 1)
                nc.scalar.activation(rms[:], lnr[:], ACT.Exp, scale=-0.5).then_inc(S("rms"), 1)
                act.wait_ge(S("hidT"), n + 1)
                for k in range(KT):
                    last = nc.scalar.activation(hT[:, k, :], bank_t[k][:], ACT.Copy, scale=g.ln1[:, k:k + 1])
                last.then_inc(S("hT"), 1)
                act.wait_ge(S("low"), n + 1)
                nc.scalar.activation(fa[:], bank_h[0][:], ACT.Copy).then_inc(S("fa"), 1)
                act.wait_ge(S("z"), n + 1)
                nc.scalar.activation(az[:], z[:], ACT.Abs).then_inc(S("az"), 1)
                act.wait_ge(S("az"), n + 1)
                nc.scalar.activation(ez[:], az[:], ACT.Exp, scale=-1.0).then_inc(S("ez"), 1)
                act.wait_ge(S("ez"), n + 1)
                nc.scalar.activation(lz[:], ez[:], ACT.Ln, bias=1.0).then_inc(S("lz"), 1)
                act.wait_ge(S("zb"), n + 1)
                nc.scalar.activation(ezb[:], zb[:], ACT.Exp).then_inc(S("ezb"), 1)
            act.wait_ge(S("sums"), 1)
            nc.scalar.activation(g.eg[:], bank[0][:, 0:H * TILES].rearrange("p (h t) -> p h t", h=H),
                                 ACT.Exp).then_inc(S("eg"), 1)

        @block.tensor
        def _(pe):
            pe.wait_ge(S("masks"), 1)
            pe.wait_ge(S("conv_in"), 48)
            for c in range(3):
                last = nc.tensor.transpose(bank[0][:, c * TAPS * H:(c + 1) * TAPS * H], conv_rows[:, c, :],
                                           g.ident[0:TAPS * H, 0:TAPS * H])
            last.then_inc(S("conv_T"), 1)
            pe.wait_ge(S("conv"), 1)
            pe.wait_ge(S("gates_in"), 16 * 11)
            pe.wait_ge(S("wb_in"), 16)
            pe.wait_ge(S("router_in"), 16)
            with pe.Fori(0, STEPS) as n:
                ffn_tensor(nc, pe, b, S, n, g.ident, bank_t, bank_c, bank_h, bank_o, lambda e: None)
                pe.wait_ge(S("hid"), n + 1)
                for k in range(KT):
                    for t in range(STEP):
                        last = nc.tensor.transpose(bank_t[k][:, t * P:(t + 1) * P], hid[:, t, k * P:(k + 1) * P],
                                                   g.ident[:])
                last.then_inc(S("hidT"), 1)
                pe.wait_ge(S("hT"), n + 1)
                for dst, w in ((bank_h[0], wfa), (bank_h[1], wga)):
                    for k in range(KT):
                        last = nc.tensor.matmul(dst[:], w[:, k, :], hT[:, k, :], start=(k == 0), stop=(k == KT - 1))
                last.then_inc(S("low"), 1)
                for t in range(STEP):
                    for k in range(KT):
                        nc.tensor.matmul(bank_c[0][:, (STEP + t) * H:(STEP + t + 1) * H], hT[:, k, t * P:(t + 1) * P],
                                         wbeta[:, k, :], start=(k == 0), stop=(k == KT - 1))
                pe.wait_ge(S("fa"), n + 1)
                for t in range(STEP):
                    last = nc.tensor.matmul(bank_c[0][:, t * H:(t + 1) * H], fa[:, t * P:(t + 1) * P], wfb[:],
                                            start=True, stop=True)
                last.then_inc(S("gates"), 1)
            pe.wait_ge(S("table"), STEPS)
            for i, part in enumerate((G_HI, G_LO)):
                last = nc.tensor.matmul(bank[0][:, 0:H * TILES], g.upto[:], g.table[:, :, part:part + TILES],
                                        start=(i == 0), stop=(i == 1))
            last.then_inc(S("sums"), 1)



CH = 4
UNITS = H * TILES // CH
PER_HEAD = TILES // CH
SLOTS = 2 * PER_HEAD
LEAD = SLOTS - 1
LOOPED = 6
BLOCKS = PER_HEAD * CH * SUBS


def stage_two(nc, g, d):
    with ExitStack() as ctx:
        def sb(name, shape, dt=F32):
            return ctx.enter_context(nc.sbuf_tensor("s2_" + name, shape, dt))

        S = Semaphores(nc, ctx, "s2_")
        Lt = [sb(f"Lt{s}", [P, CH, P]) for s in range(SLOTS)]
        QK = [sb(f"QK{s}", [P, CH, P]) for s in range(SLOTS)]
        Vn = [sb(f"Vn{s}", [P, CH, DH]) for s in range(SLOTS)]
        K1 = [sb(f"K1{s}", [P, 2, P]) for s in range(SLOTS)]
        Q1 = [sb(f"Q1{s}", [P, 2, P]) for s in range(SLOTS)]
        Kd = [sb(f"Kd{s}", [P, 2, DH]) for s in range(SLOTS)]
        cs = [sb(f"cs{s}", [P, 2 * CH]) for s in range(SLOTS)]
        w_raw = sb("w_raw", [P, 3, KT, DH])
        w_hi = [sb(f"w_hi{i}", [P, 3, KT, DH], F32R) for i in range(2)]
        w_lo = [sb(f"w_lo{i}", [P, 3, KT, DH], F32R) for i in range(2)]
        table = [sb(f"table{i}", [P, TABLE]) for i in range(2)]
        gm = [sb(f"gm_{p}", [P, CH, P], F32R) for p in ("hi", "lo")]
        conv = [sb(f"conv{i}", [P, N]) for i in range(3)]
        kT = sb("kT", [P, N])
        qT = sb("qT", [P, N])
        Pt_of = [sb(f"Pt{i}", [P, CH, P]) for i in range(2)]
        ssq = sb("ssq", [P, 2 * CH])
        lnk = sb("lnk", [P, CH])
        nk = sb("nk", [P, CH])
        rk = sb("rk", [P, CH])
        blocks = sb("blocks", [2 * BLOCKS, SUB, SUB])
        Lb, eye = blocks[0:BLOCKS], blocks[BLOCKS:]
        Tb = sb("Tb", [BLOCKS, SUB, SUB])
        Yb = sb("Yb", [BLOCKS, SUB, SUB])
        outer = sb("outer", [BLOCKS, SUB * SUB // 4])
        Y = [sb(f"Y{i}", [P, CH, P]) for i in range(2)]
        TT = [sb(f"TT{i}", [P, CH, 2 * SUB]) for i in range(2)]
        F1 = sb("F1", [P, CH, SUB])
        F2 = sb("F2", [P, CH, 2 * SUB])
        U = sb("U", [P, CH, DH])
        St = sb("St", [P, 2, DH])
        QS = sb("QS", [P, CH, DH])
        O = sb("O", [P, CH, DH])
        OG = sb("OG", [P, N])
        gT = sb("gT", [P, N])
        junk = sb("junk", [P, CH, DH])
        so = sb("so", [P, CH])
        eo = sb("eo", [P, CH])
        lno = sb("lno", [P, CH])
        fo = sb("fo", [P, CH])
        eg = [sb(f"eg{i}", [P, 2, TILES]) for i in range(2)]
        wgb = [sb(f"wgb{i}", [LOW, DH]) for i in range(2)]
        wo = [sb(f"wo{i}", [P, D]) for i in range(2)]

        bank = [ctx.enter_context(nc.psum_tensor(f"s2_bank{i}", [P, N], F32)) for i in range(8)]
        bQ, bK, bV, bD, b4, b5, b6, b7 = bank

        def by_chunk(x):
            return x[:].rearrange("p (c i) -> p c i", c=CH)

        def half(ap, second):
            return ap.rearrange("p (b c) i -> p b c i", c=2)[:, :, second, :]

        def half_column(ap, second):
            return spread(ap.rearrange("p (b c) -> p b c", c=2)[:, :, second], [P, 2, DH])

        heads = [w.rearrange("(k p) (h n) -> p k h n", p=P, n=DH) for w in (d.wq, d.wk, d.wv)]
        wgb_h = d.wgb.rearrange("p (h n) -> p h n", n=DH)
        wo_h = d.wo.rearrange("(h p) n -> p h n", p=DH)
        shape = "(z u c s r) x -> z u c s r x"
        size = dict(z=2, u=PER_HEAD, c=CH, s=SUBS, r=SUB)
        Ld, Td, Yd = (x.rearrange(shape, **size) for x in (d.l_dram, d.t_dram, d.y_dram))
        flat = [x.rearrange("(z b r) x -> z b r x", z=2, r=SUB) for x in (d.l_dram, d.t_dram, d.y_dram)]

        class Round:

            def __init__(self, i, j):
                base = 0 if i is None else i * SLOTS
                self.m, self.n = base + j, base + (j + LEAD)
                self.hm, self.hn = (x // PER_HEAD if i is None else i * 2 + x // PER_HEAD for x in (j, j + LEAD))
                self.half_m = j // 2 if i is None else i * (SLOTS // 2) + j // 2
                self.um, self.un = j % PER_HEAD, (j + LEAD) % PER_HEAD
                self.pm, self.pn = (j // PER_HEAD) % 2, ((j + LEAD) // PER_HEAD) % 2
                self.sm, self.sn = j % SLOTS, (j + LEAD) % SLOTS
                self.y = j % 2
                self.ut, self.pt, self.st = (j - 1) % PER_HEAD, ((j - 1) // PER_HEAD) % 2, (j - 1) % SLOTS
                inside = i is not None
                self.front, self.back = inside or 0 <= self.n < UNITS, inside or 0 <= self.m < UNITS
                self.tail = inside or 1 <= self.m <= UNITS
                self.load = inside or 0 <= self.m + 1 < UNITS
                self.diag = inside or 1 <= self.n <= UNITS
                self.invert = self.un < PER_HEAD - 1 and (inside or 1 <= self.hn <= H)
                self.ready_back = self.um == PER_HEAD - 1 and (inside or 0 <= self.hm + 1 < H)
                self.ready_front = self.un == 2 and (inside or 0 <= self.hn and self.hn + 1 < H)

        def rounds(eng, body):
            for m in range(-LEAD, 1):
                body(Round(None, m))
            with eng.Fori(0, LOOPED) as i:
                for j in range(1, SLOTS + 1):
                    body(Round(i, j))
            for m in range(LOOPED * SLOTS + 1, UNITS + 1):
                body(Round(None, m))

        def at(h):
            return slice(h, h + 1) if isinstance(h, int) else bass.ds(h, 1)

        block = ctx.enter_context(nc.Block())

        @block.sync
        def _(sp):
            def load_front(h):
                for i, w in enumerate(heads):
                    sp.dma_start(w_raw[:, i], w[:, :, at(h), :]).then_inc(S("w_in"), 16)

            def load_back(h, p):
                sp.dma_start(wgb[p][:], wgb_h[:, at(h), :]).then_inc(S("wo_in"), 16)
                sp.dma_start(wo[p][:], wo_h[:, at(h), :]).then_inc(S("wo_in"), 16)

            load_front(0)
            load_back(0, 0)
            sp.wait_ge(S("w_split"), 1)
            load_front(1)
            sp.wait_ge(S("blank"), 1)
            sp.wait_ge(S("eye"), 2)

            def body(r):
                more_front = r.un == 3 and (not isinstance(r.hn, int) or 0 <= r.hn and r.hn + 2 < H)
                more_back = r.um == 2 and (not isinstance(r.hm, int) or 0 <= r.hm and r.hm + 1 < H)
                if more_front and not r.diag:
                    sp.wait_ge(S("w_split"), r.hn + 2)
                if more_back and not r.diag:
                    sp.wait_ge(S("proj"), r.m - 1)
                if r.diag:
                    sp.wait_ge(S("Lt"), r.n)
                    slot, u, z = (r.sn - 1) % SLOTS, (r.un - 1) % PER_HEAD, r.pn if r.un else 1 - r.pn
                    for s in range(SUBS):
                        sub = slice(s * SUB, (s + 1) * SUB)
                        if s == 1 and more_front:
                            sp.wait_ge(S("w_split"), r.hn + 2)
                        if s == 2 and more_back:
                            sp.wait_ge(S("proj"), r.m - 1)
                        sp.dma_start(Ld[z, u, :, s].rearrange("c r x -> r c x"), Lt[slot][sub, :, sub]
                                     ).then_inc(S("l_out"), 16)
                    if r.un == 0:
                        sp.wait_ge(S("l_out"), r.n * (16 * SUBS))
                        sp.dma_start(Lb, flat[0][1 - r.pn]).then_inc(S("lb_in"), 16)
                        sp.dma_start(Tb[:], eye).then_inc(S("lb_in"), 16)
                if more_front:
                    load_front(r.hn + 2)
                if more_back:
                    load_back(r.hm + 1, 1 - r.pm)
                if r.invert and r.un == 2:
                    sp.wait_ge(S("inverted"), r.hn)
                    sp.dma_start(flat[1][1 - r.pn], Tb[:]).then_inc(S("ty_out"), 16)
                    if r.load:
                        wait(sp, S("W1"), r.m)
                    sp.dma_start(flat[2][1 - r.pn], Yb[:]).then_inc(S("ty_out"), 16)
                    sp.wait_ge(S("ty_out"), r.hn * 32)
                if r.load:
                    u, z, y = (r.um + 1) % PER_HEAD, r.pm if r.um < 3 else 1 - r.pm, 1 - r.y
                    if not (r.invert and r.un == 2):
                        wait(sp, S("W1"), r.m)
                    for s, (row, col) in enumerate(((0, 0), (SUB, SUB), (2 * SUB, 0))):
                        sp.dma_start(TT[y][row:row + SUB, :, col:col + SUB], Td[z, u, :, s].rearrange("c r x -> r c x")
                                     ).then_inc(S(f"y_in{y}"), 16)
                    for s in range(SUBS):
                        sub = slice(s * SUB, (s + 1) * SUB)
                        sp.dma_start(Y[y][sub, :, sub], Yd[z, u, :, s].rearrange("c r x -> r c x")
                                     ).then_inc(S(f"y_in{y}"), 16)

            rounds(sp, body)

        @block.gpsimd
        def _(pool):
            nc.gpsimd.memset(eye, 0.0).then_inc(S("eye"), 1)
            pool.wait_ge(S("eye"), 1)
            nc.gpsimd.affine_select(out=eye, in_=eye, compare_op=ALU.not_equal, fill=1.0, base=0,
                                    pattern=[[1, SUB], [-1, SUB]], channel_multiplier=0).then_inc(S("eye"), 1)
            pool.wait_ge(S("eye"), 2)
            cuts = (0, 11, 21, SUB - 1)
            per_head = 2 * (SUB - 1)

            def masked(u, p):
                for part, col in enumerate((G_HI, G_LO)):
                    last = nc.gpsimd.tensor_tensor(gm[part][:], spread(g.upto[:, :], [P, CH, P], 1),
                                                   spread(table[p][:, col + u * CH:col + (u + 1) * CH], [P, CH, P]),
                                                   ALU.mult)
                last.then_inc(S("gm"), 1)

            pool.wait_ge(S("table"), 1)
            masked(0, 0)

            def body(r):
                if r.front and not (isinstance(r.n, int) and r.n + 1 == UNITS):
                    if r.un == 3:
                        pool.wait_ge(S("table"), r.hn + 2)
                    pool.wait_ge(S("D"), r.n + 1)
                    masked((r.un + 1) % PER_HEAD, r.pn if r.un < 3 else 1 - r.pn)
                if r.invert:
                    head = r.hn - 1
                    if r.un == 0:
                        pool.wait_ge(S("lb_in"), r.hn * 32)
                    for j in range(cuts[r.un], cuts[r.un + 1]):
                        shape = [BLOCKS, SUB - 1 - j, j + 1]
                        terms = outer[:, 0:shape[1] * shape[2]].rearrange("b (i x) -> b i x", i=shape[1])
                        if j > 0:
                            pool.wait_ge(S("inv"), head * per_head + 2 * j)
                        nc.gpsimd.tensor_tensor(terms, spread(Lb[:, j, j + 1:], shape), spread(Tb[:, j, 0:j + 1], shape, 1),
                                                ALU.mult).then_inc(S("inv"), 1)
                        pool.wait_ge(S("inv"), head * per_head + (2 * j + 1))
                        nc.gpsimd.tensor_tensor(Tb[:, j + 1:, 0:j + 1], Tb[:, j + 1:, 0:j + 1], terms,
                                                ALU.subtract).then_inc(S("inv"), 1)
                    if r.un == 2:
                        pool.wait_ge(S("inv"), head * per_head + per_head)
                        nc.gpsimd.tensor_tensor(Yb[:], Tb[:].rearrange("b r c -> b c r"),
                                                spread(g.ones[0:BLOCKS, 0:1], [BLOCKS, SUB, SUB]), ALU.mult
                                                ).then_inc(S("inverted"), 1)

            rounds(pool, body)

        @block.vector
        def _(dve):
            def ready_front(h, p):
                nc.vector.tensor_scalar(table[p][:].unsqueeze(1), g.table[:, at(h), :], 1.0, None, ALU.mult
                                        ).then_inc(S("table"), 1)
                dve.wait_ge(S("w_in"), h * 48 + 48)
                nc.vector.tensor_copy(w_hi[p][:], w_raw[:]).then_inc(S("w_hi"), 1)
                dve.wait_ge(S("w_hi"), h + 1)
                nc.vector.tensor_tensor(w_lo[p][:], w_raw[:], w_hi[p][:].bitcast(F32), ALU.subtract
                                        ).then_inc(S("w_split"), 1)

            def ready_back(h, p):
                for k, src in enumerate((g.eg, g.neg_eg)):
                    last = nc.vector.tensor_scalar(eg[p][:, k:k + 1, :], src[:, at(h), :], 1.0, None, ALU.mult)
                dve.wait_ge(S("wo_in"), h * 32 + 32)
                nc.vector.tensor_scalar(wo[p][:], wo[p][:], g.onorm[:, 0:1], None, ALU.mult
                                        ).then_inc(S("wo_ready"), 1)

            for x in (Y[0], Y[1], TT[0], TT[1], QS):
                last = nc.vector.memset(x[:], 0.0)
            last.then_inc(S("blank"), 1)
            nc.vector.memset(fo[:], 0.0).then_inc(S("acc"), 1)
            ready_front(0, 0)

            def taps(r, c, ps, which):
                if which[0] == 1:
                    dve.wait_ge(S("tap"), r.n * 3 + (c + 1))
                for s in which:
                    out = conv[c][:].rearrange("p (b t) -> p b t", b=2)[:, :, s:]
                    if s > 1:
                        dve.wait_ge(S("taps"), r.n * 9 + (3 * c + s - 1))
                    nc.vector.scalar_tensor_tensor(
                        out=out, in0=ps[:].rearrange("p (b t) -> p b t", b=2)[:, :, 0:T - s],
                        scalar=table[r.pn][:, CONV + TAPS * c + 3 - s:CONV + TAPS * c + 4 - s],
                        in1=out, op0=ALU.mult, op1=ALU.add).then_inc(S("taps"), 1)

            def body(r):
                Pt = Pt_of[r.sn % 2]
                if r.front:
                    taps(r, 0, bQ, (1, 2, 3))
                if r.tail:
                    dve.wait_ge(S("KS"), r.m)
                    for c in (1, 3):
                        tile = r.ut * CH + c
                        last = nc.vector.scalar_tensor_tensor(
                            out=Vn[r.st][:, c, :], in0=b6[:, c * DH:(c + 1) * DH], scalar=eg[r.pt][:, 1, tile:tile + 1],
                            in1=Vn[r.st][:, c, :], op0=ALU.mult, op1=ALU.add)
                    last.then_inc(S("R1"), 1)
                if r.front:
                    taps(r, 1, bK, (1, 2, 3))
                if r.tail:
                    dve.wait_ge(S("W1"), r.m)
                    nc.vector.tensor_tensor(half(U[:], 1), half(by_chunk(b5), 1), half_column(cs[r.st][:, 0:CH], 1),
                                            ALU.mult).then_inc(S("U1"), 1)
                if r.front:
                    taps(r, 2, bV, (1, 2))
                if r.tail:
                    dve.wait_ge(S("QSo"), r.m)
                    dve.wait_ge(S("Om"), r.m)
                    nc.vector.tensor_tensor(O[:], by_chunk(b6), QS[:], ALU.add).then_inc(S("O"), 1)
                if r.front:
                    taps(r, 2, bV, (3,))
                if r.back:
                    dve.wait_ge(S("W0"), r.m + 1)
                    nc.vector.tensor_tensor(half(U[:], 0), half(by_chunk(b5), 0), half_column(cs[r.sm][:, 0:CH], 0),
                                            ALU.mult).then_inc(S("U0"), 1)
                if r.tail:
                    dve.wait_ge(S("OT"), r.m)
                    dve.wait_ge(S("gT"), r.m)
                    nc.vector.tensor_tensor(OG[:], b7[:], gT[:], ALU.mult).then_inc(S("OG"), 1)
                if r.front:
                    dve.wait_ge(S("qk"), r.n + 1)
                    nc.vector.tensor_copy(K1[r.sn][:], half(by_chunk(kT), 1))
                    nc.vector.tensor_copy(Q1[r.sn][:], half(by_chunk(qT), 1))
                if r.tail:
                    dve.wait_ge(S("so"), r.m)
                    nc.vector.scalar_tensor_tensor(out=eo[:], in0=so[:], scalar=1.0 / DH,
                                                   in1=cs[r.st][:, CH:2 * CH], op0=ALU.mult,
                                                   op1=ALU.add).then_inc(S("eo"), 1)
                if r.front:
                    dve.wait_ge(S("ssq"), r.n + 1)
                    nc.vector.tensor_scalar(ssq[:], bD[:, 2 * DH:2 * DH + 2 * CH], EPS, None, ALU.add
                                            ).then_inc(S("norms"), 1)
                    nc.vector.tensor_tensor(Kd[r.sn][:], bD[:, 0:2 * DH].rearrange("p (b i) -> p b i", b=2),
                                            half(Pt[:], 0)[:, :, P - 1:P].to_broadcast([P, 2, DH]), ALU.mult
                                            ).then_inc(S("Kd"), 1)
                    dve.wait_ge(S("norms"), r.n + 1)
                    nc.vector.reciprocal(rk[:], ssq[:, 0:CH]).then_inc(S("rk"), 1)
                    nc.vector.tensor_scalar(cs[r.sn][:, CH:2 * CH], ssq[:, CH:2 * CH], float(DH) * EPS, None, ALU.mult)
                    dve.wait_ge(S("rk"), r.n + 1)
                    nc.vector.tensor_tensor(cs[r.sn][:, 0:CH], rk[:],
                                            table[r.pn][:, BETA + r.un * CH:BETA + (r.un + 1) * CH], ALU.mult
                                            ).then_inc(S("c"), 1)
                    dve.wait_ge(S("KK"), r.n + 1)
                    dve.wait_ge(S("c"), r.n + 1)
                    for c in range(CH):
                        last = nc.vector.scalar_tensor_tensor(
                            out=Lt[r.sn][:, c, :], in0=bQ[:, c * P:(c + 1) * P], scalar=cs[r.sn][:, c:c + 1],
                            in1=Pt[:, c, :], op0=ALU.mult, op1=ALU.mult)
                    last.then_inc(S("Lt"), 1)
                    dve.wait_ge(S("KQ"), r.n + 1)
                    nc.vector.tensor_tensor(QK[r.sn][:], by_chunk(bK), Pt[:], ALU.mult).then_inc(S("QK"), 1)
                    dve.wait_ge(S("nk"), r.n + 1)
                    dve.wait_ge(S("vT"), r.n + 1)
                    nc.vector.tensor_tensor(Vn[r.sn][:], by_chunk(bV), spread(nk[:, :], [P, CH, DH]), ALU.mult
                                            ).then_inc(S("Vn"), 1)
                if r.tail:
                    dve.wait_ge(S("fo"), r.m)
                    dve.wait_ge(S("proj"), r.m)
                    for c in range(CH):
                        tile = g.acc[:, r.ut * CH + c, :]
                        ps = (b6, b7)[c // 2][:, (c % 2) * D:(c % 2 + 1) * D]
                        last = nc.vector.scalar_tensor_tensor(out=tile, in0=ps, scalar=fo[:, c:c + 1], in1=tile,
                                                              op0=ALU.mult, op1=ALU.add)
                    last.then_inc(S("acc"), 1)
                if r.front and r.ready_front:
                    ready_front(r.hn + 1, 1 - r.pn)
                if r.ready_back:
                    ready_back(r.hm + 1, 1 - r.pm)

            rounds(dve, body)

        @block.scalar
        def _(act):
            def tap(r, c, ps):
                act.wait_ge(S("qkv"), r.n * 3 + (c + 1))
                nc.scalar.activation(conv[c][:], ps[:], ACT.Copy,
                                     scale=table[r.pn][:, CONV + TAPS * c + 3:CONV + TAPS * c + 4]
                                     ).then_inc(S("tap"), 1)

            def body(r):
                Pt = Pt_of[r.sn % 2]
                if r.front:
                    act.wait_ge(S("D"), r.n + 1)
                    nc.scalar.activation(Pt[:], by_chunk(bD), ACT.Exp).then_inc(S("Pt"), 1)
                    if r.un == 0:
                        act.wait_ge(S("table"), r.hn + 1)
                    tap(r, 0, bQ)
                if r.tail:
                    act.wait_ge(S("QSm"), r.m)
                    for c in (1, 3):
                        tile = r.ut * CH + c
                        last = nc.scalar.activation(QS[:, c, :], b7[:, c * DH:(c + 1) * DH], ACT.Copy,
                                                    scale=eg[r.pt][:, 0, tile:tile + 1])
                    last.then_inc(S("QSo"), 1)
                if r.front:
                    tap(r, 1, bK)
                if r.back:
                    act.wait_ge(S("F"), r.m + 1)
                    nc.scalar.activation(F1[SUB:2 * SUB], b4[SUB:2 * SUB, 0:CH * SUB].rearrange(
                        "p (c i) -> p c i", c=CH), ACT.Copy)
                    nc.scalar.activation(F1[3 * SUB:], b4[3 * SUB:, 0:CH * SUB].rearrange(
                        "p (c i) -> p c i", c=CH), ACT.Copy).then_inc(S("F1"), 1)
                if r.front:
                    tap(r, 2, bV)
                if r.back:
                    act.wait_ge(S("X"), r.m + 1)
                    for q in (0, 2):
                        nc.scalar.activation(Y[r.y][q * SUB:(q + 1) * SUB, :, (q + 1) * SUB:(q + 2) * SUB],
                                             b4[q * SUB:(q + 1) * SUB, 0:CH * SUB].rearrange("p (c i) -> p c i", c=CH),
                                             ACT.Copy, scale=-1.0)
                    nc.scalar.activation(TT[r.y][SUB:2 * SUB, :, 0:SUB],
                                         b4[SUB:2 * SUB, CH * SUB:2 * CH * SUB].rearrange("p (c i) -> p c i", c=CH),
                                         ACT.Copy, scale=-1.0).then_inc(S("merged"), 1)
                if r.front or r.back:
                    nc.scalar.preload_act_table_set(SILU)
                if r.back:
                    act.wait_ge(S("F'"), r.m + 1)
                    nc.scalar.activation(F2[2 * SUB:], b4[2 * SUB:, 0:CH * 2 * SUB].rearrange("p (c i) -> p c i", c=CH),
                                         ACT.Copy).then_inc(S("F2"), 1)
                if r.front:
                    act.wait_ge(S("taps"), r.n * 9 + 3)
                    nc.scalar.activation(qT[:], conv[0][:], ACT.Silu)
                if r.back:
                    act.wait_ge(S("X'"), r.m + 1)
                    nc.scalar.activation(Y[r.y][0:2 * SUB, :, 2 * SUB:], b4[0:2 * SUB, 0:CH * 2 * SUB].rearrange(
                        "p (c i) -> p c i", c=CH), ACT.Copy, scale=-1.0).then_inc(S("Y"), 1)
                if r.front:
                    act.wait_ge(S("taps"), r.n * 9 + 6)
                    nc.scalar.activation(kT[:], conv[1][:], ACT.Silu).then_inc(S("qk"), 1)
                    act.wait_ge(S("qk"), r.n + 1)
                    nc.scalar.activation(conv[1][:], kT[:], ACT.Square)
                    nc.scalar.activation(conv[0][:], qT[:], ACT.Square).then_inc(S("squares"), 1)
                if r.tail:
                    act.wait_ge(S("O"), r.m)
                    for c in range(CH):
                        last = nc.scalar.activation(junk[:, c, :], O[:, c, :], ACT.Square, accum_out=so[:, c:c + 1])
                    last.then_inc(S("so"), 1)
                if r.front:
                    act.wait_ge(S("taps"), r.n * 9 + 9)
                    nc.scalar.activation(conv[2][:], conv[2][:], ACT.Silu).then_inc(S("v"), 1)
                if r.back:
                    wait(act, S("OG"), r.m)
                    act.wait_ge(S("gate"), r.m + 1)
                    nc.scalar.activation(gT[:], b4[:], ACT.Silu).then_inc(S("gT"), 1)
                nc.scalar.preload_act_table_set(LOG_EXP)
                if r.back:
                    act.wait_ge(S("S"), r.m + 1)
                    nc.scalar.activation(St[:], half(by_chunk(b5), 1), ACT.Copy).then_inc(S("St"), 1)
                if r.front:
                    act.wait_ge(S("norms"), r.n + 1)
                    nc.scalar.activation(lnk[:], ssq[:, 0:CH], ACT.Ln).then_inc(S("lnk"), 1)
                if r.tail:
                    act.wait_ge(S("eo"), r.m)
                    nc.scalar.activation(lno[:], eo[:], ACT.Ln).then_inc(S("lno"), 1)
                if r.front:
                    act.wait_ge(S("lnk"), r.n + 1)
                    nc.scalar.activation(nk[:], lnk[:], ACT.Exp, scale=0.5).then_inc(S("nk"), 1)
                if r.tail:
                    act.wait_ge(S("lno"), r.m)
                    nc.scalar.activation(fo[:], lno[:], ACT.Exp, scale=-0.5).then_inc(S("fo"), 1)

            rounds(act, body)

        @block.tensor
        def _(pe):
            def project(r, c, ps, before_last=None):
                cols = slice(r.un * N, (r.un + 1) * N)
                parts = [(w, x, k) for w, x in ((w_hi, g.hT_hi), (w_hi, g.hT_lo), (w_lo, g.hT_hi)) for k in range(KT)]
                for i, (w, x, k) in enumerate(parts):
                    if i == len(parts) - 1 and before_last:
                        before_last()
                    last = nc.tensor.matmul(ps[:], w[r.pn][:, c, k, :], x[:, k, cols], start=(i == 0),
                                            stop=(i == len(parts) - 1))
                last.then_inc(S("qkv"), 1)

            def body(r):
                y_in = (S(f"y_in{r.y}"), r.half_m * 112 + 112)
                up, low = slice(0, 2 * SUB), slice(2 * SUB, P)
                if r.front:
                    pe.wait_ge(S("gm"), r.n + 1)
                    wait(pe, S("Kd"), r.n)
                    nc.tensor.matmul(bD[:], g.after_r[:], gm[0][:], start=True, stop=False)
                    nc.tensor.matmul(bD[:], g.after_r[:], gm[1][:], start=False, stop=False)
                    nc.tensor.matmul(bD[:], g.ident_r[:], spread(g.far_r[:, :], [P, CH, P], 1), start=False,
                                     stop=True).then_inc(S("D"), 1)
                    if r.un == 0:
                        pe.wait_ge(S("w_split"), r.hn + 1)
                    wait(pe, S("Lt"), r.n)
                    project(r, 0, bQ)
                if r.tail:
                    pe.wait_ge(S("acc"), r.m)
                    pe.wait_ge(S("St"), r.m)
                    for dst, x, sem in ((b6, K1, "KS"), (b7, Q1, "QSm")):
                        for i, c in enumerate((1, 3)):
                            last = nc.tensor.matmul(dst[:, c * DH:(c + 1) * DH], x[r.st][:, i, :], St[:, i, :],
                                                    start=True, stop=True)
                        last.then_inc(S(sem), 1)

                def merge_ready():
                    if r.back:
                        pe.wait_ge(*y_in)
                        wait(pe, S("gT"), r.m)
                if r.front:
                    wait(pe, S("QK"), r.n)
                    project(r, 1, bK, merge_ready)
                else:
                    merge_ready()
                if r.back:
                    for c in range(CH):
                        for q in (0, 2):
                            rows, below = slice(q * SUB, (q + 1) * SUB), slice((q + 1) * SUB, (q + 2) * SUB)
                            last = nc.tensor.matmul(b4[below, c * SUB:(c + 1) * SUB], Lt[r.sm][rows, c, below],
                                                    TT[r.y][rows, c, 0:SUB], start=True, stop=True,
                                                    tile_position=(q * SUB, (q + 1) * SUB))
                    last.then_inc(S("F"), 1)

                def f1_ready():
                    if r.back:
                        pe.wait_ge(S("F1"), r.m + 1)
                if r.front:
                    wait(pe, S("Vn"), r.n)
                    project(r, 2, bV, f1_ready)
                else:
                    f1_ready()
                if r.back:
                    for c in range(CH):
                        for q in (0, 2):
                            rows, below = slice(q * SUB, (q + 1) * SUB), slice((q + 1) * SUB, (q + 2) * SUB)
                            nc.tensor.matmul(b4[rows, c * SUB:(c + 1) * SUB], F1[below, c, :], Y[r.y][below, c, below],
                                             start=True, stop=True, tile_position=((q + 1) * SUB, q * SUB))
                        second = slice(SUB, 2 * SUB)
                        last = nc.tensor.matmul(b4[second, (CH + c) * SUB:(CH + c + 1) * SUB], Y[r.y][second, c, second],
                                                F1[second, c, :], start=True, stop=True, tile_position=(SUB, SUB))
                    last.then_inc(S("X"), 1)
                if r.tail:
                    pe.wait_ge(S("R1"), r.m)
                    for c in (1, 3):
                        if c == 3 and r.back:
                            pe.wait_ge(S("merged"), r.m + 1)
                        last = nc.tensor.matmul(b5[:, c * DH:(c + 1) * DH], Y[1 - r.y][:, c, :], Vn[r.st][:, c, :],
                                                start=True, stop=True)
                    last.then_inc(S("W1"), 1)
                elif r.back:
                    pe.wait_ge(S("merged"), r.m + 1)
                if r.back:
                    for c in range(CH):
                        last = nc.tensor.matmul(b4[low, c * 2 * SUB:(c + 1) * 2 * SUB], Lt[r.sm][up, c, low],
                                                TT[r.y][up, c, :], start=True, stop=True, tile_position=(0, 2 * SUB))
                    last.then_inc(S("F'"), 1)
                if r.tail:
                    pe.wait_ge(S("U1"), r.m)
                    for c in range(CH):
                        if c == CH - 1 and r.back:
                            pe.wait_ge(S("F2"), r.m + 1)
                        last = nc.tensor.matmul(b6[:, c * DH:(c + 1) * DH], QK[r.st][:, c, :], U[:, c, :],
                                                start=True, stop=True)
                    last.then_inc(S("Om"), 1)
                elif r.back:
                    pe.wait_ge(S("F2"), r.m + 1)
                if r.back:
                    for c in range(CH):
                        last = nc.tensor.matmul(b4[up, c * 2 * SUB:(c + 1) * 2 * SUB], F2[low, c, :],
                                                Y[r.y][low, c, low], start=True, stop=True, tile_position=(2 * SUB, 0))
                    last.then_inc(S("X'"), 1)
                if r.tail:
                    pe.wait_ge(S("O"), r.m)
                    for c in range(CH):
                        last = nc.tensor.transpose(b7[:, c * P:(c + 1) * P], O[:, c, :], g.ident[:])
                    last.then_inc(S("OT"), 1)
                if r.back:
                    pe.wait_ge(S("Y"), r.m + 1)
                    for c in (0, 2):
                        last = nc.tensor.matmul(b5[:, c * DH:(c + 1) * DH], Y[r.y][:, c, :], Vn[r.sm][:, c, :],
                                                start=True, stop=True)
                    last.then_inc(S("W0"), 1)
                if r.front:
                    pe.wait_ge(S("qk"), r.n + 1)
                    for c in range(CH):
                        cols = slice(c * P, (c + 1) * P)
                        last = nc.tensor.matmul(bQ[:, cols], kT[:, cols], kT[:, cols], start=True, stop=True)
                    last.then_inc(S("KK"), 1)
                if r.back:
                    if r.um == 0:
                        pe.wait_ge(S("wo_ready"), r.hm + 1)
                    nc.tensor.matmul(b4[:], wgb[r.pm][:], g.gateT[:, r.um * N:(r.um + 1) * N], start=True,
                                     stop=True).then_inc(S("gate"), 1)
                if r.front:
                    pe.wait_ge(S("squares"), r.n + 1)
                    for i, c in enumerate((0, 2)):
                        nc.tensor.transpose(bD[:, i * P:(i + 1) * P], kT[:, c * P:(c + 1) * P], g.ident[:])
                    for i, x in enumerate((conv[1], conv[0])):
                        for c in range(CH):
                            col = 2 * P + i * CH + c
                            last = nc.tensor.matmul(bD[:, col:col + 1], x[:, c * P:(c + 1) * P], g.ones[:, 0:1],
                                                    start=True, stop=True)
                    last.then_inc(S("ssq"), 1)
                if r.back:
                    pe.wait_ge(S("U0"), r.m + 1)
                    for i, c in enumerate((0, 2)):
                        last = nc.tensor.matmul(b5[:, (c + 1) * DH:(c + 2) * DH], Kd[r.sm][:, i, :], U[:, c, :],
                                                start=True, stop=True)
                    last.then_inc(S("S"), 1)
                if r.front:
                    for c in range(CH):
                        cols = slice(c * P, (c + 1) * P)
                        last = nc.tensor.matmul(bK[:, cols], kT[:, cols], qT[:, cols], start=True, stop=True)
                    last.then_inc(S("KQ"), 1)
                    pe.wait_ge(S("v"), r.n + 1)
                    for c in range(CH):
                        last = nc.tensor.transpose(bV[:, c * P:(c + 1) * P], conv[2][:, c * P:(c + 1) * P], g.ident[:])
                    last.then_inc(S("vT"), 1)
                if r.tail:
                    pe.wait_ge(S("OG"), r.m)
                    for c in range(CH):
                        last = nc.tensor.matmul((b6, b7)[c // 2][:, (c % 2) * D:(c % 2 + 1) * D],
                                                OG[:, c * P:(c + 1) * P], wo[r.pt][:], start=True, stop=True)
                    last.then_inc(S("proj"), 1)

            rounds(pe, body)



def stage_three(nc, g, d):
    with ExitStack() as ctx:
        def sb(name, shape, dt=F32):
            return ctx.enter_context(nc.sbuf_tensor("s3_" + name, shape, dt))

        S = Semaphores(nc, ctx, "s3_")
        b = ffn_buffers(nc, ctx, "s3_")
        raw = sb("raw", [P, KT, INNER])
        w_gate = [sb(f"gate_{p}", [P, KT, INNER], F32R) for p in ("hi", "lo")]
        w_up = [sb(f"up_{p}", [P, KT, INNER], F32R) for p in ("hi", "lo")]
        w_down = sb("down", [P, INNER // P, D])
        x1 = sb("x1", [P, STEP, D])
        x2 = sb("x2", [P, STEP, D])
        out = sb("out", [P, STEP, D])
        h2 = sb("h2", [P, STEP, D])
        h2T = sb("h2T", [P, KT, N])
        squares = sb("squares", [P, STEP, D])
        ms = sb("ms", [P, STEP])
        lnm = sb("lnm", [P, STEP])
        rms = sb("rms", [P, STEP])
        act_g = [sb(f"act_g{i}", [P, N]) for i in range(2)]
        act_m = [sb(f"act_m{i}", [P, N]) for i in range(2)]

        bank = [ctx.enter_context(nc.psum_tensor(f"s3_bank{i}", [P, N], F32)) for i in range(8)]
        bank_t, bank_c, bank_h, bank_o = bank[0:2], bank[2:4], bank[4:6], bank[6:8]
        x1_tiles = d.x1_dram.rearrange("(n p) d -> p n d", p=P)
        out_tiles = d.out.rearrange("b (c p) d -> p (b c) d", p=P)
        NM = INNER // P
        block = ctx.enter_context(nc.Block())

        @block.sync
        def _(sp):
            sp.dma_start(x1[:], x1_tiles[:, 0:STEP, :]).then_inc(S("moved"), 16)
            sp.dma_start(raw[:], d.w_gate.rearrange("(k p) n -> p k n", p=P)).then_inc(S("mlp_in"), 16)
            ffn_load(sp, b, S, d.router_w, d.Wa, d.Wb)
            sp.dma_start(w_down[:], d.w_down.rearrange("(m p) n -> p m n", p=P)).then_inc(S("down_in"), 16)
            sp.wait_ge(S("gate_split"), 1)
            sp.dma_start(raw[:], d.w_up.rearrange("(k p) n -> p k n", p=P)).then_inc(S("mlp_in"), 16)
            with sp.Fori(0, STEPS - 1) as n:
                sp.wait_ge(S("out"), n + 1)
                sp.dma_start(x1[:], x1_tiles[:, bass.ds(n * STEP + STEP, STEP), :]).then_inc(S("moved"), 16)
                sp.dma_start(out_tiles[:, bass.ds(n * STEP, STEP), :], out[:]).then_inc(S("moved"), 16)
            sp.wait_ge(S("out"), STEPS)
            sp.dma_start(out_tiles[:, TILES - STEP:TILES, :], out[:]).then_inc(S("moved"), 16)
            sp.wait_ge(S("moved"), 32 * STEPS)

        @block.gpsimd
        def _(pool):
            ffn_constants_pool(nc, pool, b, S)

        @block.vector
        def _(dve):
            for i, w in enumerate((w_gate, w_up)):
                dve.wait_ge(S("mlp_in"), 16 * (i + 1))
                nc.vector.tensor_copy(w[0][:], raw[:]).then_inc(S("mlp_hi"), 1)
                dve.wait_ge(S("mlp_hi"), i + 1)
                nc.vector.tensor_tensor(w[1][:], raw[:], w[0][:].bitcast(F32), ALU.subtract
                                        ).then_inc(S("gate_split" if i == 0 else "up_split"), 1)
                if i == 0:
                    ffn_constants_vector(nc, dve, b, S)
            with dve.Fori(0, STEPS) as n:
                dve.wait_ge(S("rms"), n + 1)
                for t in range(STEP):
                    last = nc.vector.tensor_scalar(h2[:, t:t + 1, :], g.acc[:, bass.ds(n * STEP + t, 1), :], rms[:, t:t + 1],
                                                   None, ALU.mult)
                last.then_inc(S("h2"), 1)
                dve.wait_ge(S("h2T"), n + 1)
                nc.vector.tensor_copy(b.xnT_hi[:], h2T[:]).then_inc(S("h2T_hi"), 1)
                dve.wait_ge(S("h2T_hi"), n + 1)
                nc.vector.tensor_tensor(b.xnT_lo[:], h2T[:], b.xnT_hi[:].bitcast(F32), ALU.subtract
                                        ).then_inc(S("h2T_lo"), 1)
                for m in range(NM):
                    dve.wait_ge(S("silu"), n * NM + m + 1)
                    if m >= 2:
                        dve.wait_ge(S("mdown"), n * NM + m - 1)
                    nc.vector.tensor_tensor(act_m[m % 2][:], bank_c[m % 2][:], act_g[m % 2][:],
                                            ALU.mult).then_inc(S("act_m"), 1)
                dve.wait_ge(S("moved"), n * 32 + 16)
                nc.vector.tensor_tensor(x2[:], x1[:], g.acc[:, bass.ds(n * STEP, STEP), :], ALU.add
                                        ).then_inc(S("x12"), 1)
                dve.wait_ge(S("x12"), n + 1)
                dve.wait_ge(S("mdown"), n * NM + NM)
                for i in range(2):
                    last = nc.vector.tensor_tensor(x2[:, 2 * i:2 * i + 2, :], x2[:, 2 * i:2 * i + 2, :],
                                                   bank_o[i][:].rearrange("p (t d) -> p t d", t=2), ALU.add)
                last.then_inc(S("x2"), 1)
                ffn_vector_front(nc, dve, b, S, n, x2, bank_c[0], lambda e: e.wait_ge(S("x2"), n + 1))
                ffn_vector_experts(nc, dve, b, S, n, bank_h)
                dve.wait_ge(S("down"), n * NE + NE)
                for i in range(2):
                    last = nc.vector.tensor_tensor(out[:, 2 * i:2 * i + 2, :], bank_o[i][:].rearrange("p (t d) -> p t d", t=2),
                                                   x2[:, 2 * i:2 * i + 2, :], ALU.add)
                last.then_inc(S("out"), 1)

        @block.scalar
        def _(act):
            with act.Fori(0, STEPS) as n:
                nc.scalar.preload_act_table_set(LOG_EXP)
                for t in range(STEP):
                    last = nc.scalar.activation(squares[:, t:t + 1, :], g.acc[:, bass.ds(n * STEP + t, 1), :], ACT.Square,
                                                accum_out=ms[:, t:t + 1])
                last.then_inc(S("ms"), 1)
                act.wait_ge(S("ms"), n + 1)
                nc.scalar.activation(lnm[:], ms[:], ACT.Ln, scale=1.0 / D, bias=EPS).then_inc(S("lnm"), 1)
                act.wait_ge(S("lnm"), n + 1)
                nc.scalar.activation(rms[:], lnm[:], ACT.Exp, scale=-0.5).then_inc(S("rms"), 1)
                act.wait_ge(S("h2x"), n + 1)
                for k in range(KT):
                    last = nc.scalar.activation(h2T[:, k, :], bank_t[k][:], ACT.Copy, scale=g.ln2[:, k:k + 1])
                last.then_inc(S("h2T"), 1)
                for m in range(NM):
                    act.wait_ge(S("mup"), n * NM + m + 1)
                    if m >= 2:
                        act.wait_ge(S("act_m"), n * NM + m - 1)
                    nc.scalar.activation(act_g[m % 2][:], bank_h[m % 2][:], ACT.Silu).then_inc(S("silu"), 1)
                ffn_scalar(nc, act, b, S, n, bank_t, bank_c)

        @block.tensor
        def _(pe):
            pe.wait_ge(S("wb_in"), 16)
            pe.wait_ge(S("router_in"), 16)
            pe.wait_ge(S("down_in"), 16)
            with pe.Fori(0, STEPS) as n:
                pe.wait_ge(S("h2"), n + 1)
                for k in range(KT):
                    for t in range(STEP):
                        last = nc.tensor.transpose(bank_t[k][:, t * P:(t + 1) * P], h2[:, t, k * P:(k + 1) * P], g.ident[:])
                last.then_inc(S("h2x"), 1)

                def up(m):
                    cols = slice(m * P, (m + 1) * P)
                    for dst, w in ((bank_h[m % 2], w_gate), (bank_c[m % 2], w_up)):
                        parts = [(u, x, k) for u, x in ((w[0], b.xnT_hi), (w[0], b.xnT_lo), (w[1], b.xnT_hi))
                                 for k in range(KT)]
                        for i, (u, x, k) in enumerate(parts):
                            last = nc.tensor.matmul(dst[:], u[:, k, cols], x[:, k, :], start=(i == 0),
                                                    stop=(i == len(parts) - 1))
                    last.then_inc(S("mup"), 1)

                pe.wait_ge(S("h2T_lo"), n + 1)
                up(0)
                up(1)
                for m in range(NM):
                    pe.wait_ge(S("act_m"), n * NM + m + 1)
                    for t in range(STEP):
                        last = nc.tensor.matmul(bank_o[t // 2][:, (t % 2) * D:(t % 2 + 1) * D],
                                                act_m[m % 2][:, t * P:(t + 1) * P], w_down[:, m, :],
                                                start=(m == 0 and t % 2 == 0), stop=(m == NM - 1),
                                                skip_group_check=True)
                    last.then_inc(S("mdown"), 1)
                    if m + 2 < NM:
                        up(m + 2)
                ffn_tensor(nc, pe, b, S, n, g.ident, bank_t, bank_c, bank_h, bank_o, lambda e: None)


def program(nc, d):
    with ExitStack() as ctx:
        g = persistent_buffers(nc, ctx)
        with ExitStack() as attention:
            attention_buffers(nc, attention, g)
            stage_one(nc, g, d)
            stage_two(nc, g, d)
        stage_three(nc, g, d)


_INS = ['x', 'wq', 'wk', 'wv', 'conv_q', 'conv_k', 'conv_v', 'wfa', 'wfb', 'wb', 'wga', 'wgb', 'a_log', 'dt_bias',
        'o_norm_w', 'wo', 'ln1_w', 'ln2_w', 'w_gate', 'w_up', 'w_down']
_FFN_INS = ['router_w', 'Wa', 'Wb']


class _Dram:
    pass


def kernel(**inputs):
    import numpy as _np
    import concourse.bacc as _bacc
    from concourse import mybir as _mybir
    from concourse.bass_utils import run_bass_kernel_spmd as _run

    nc = _bacc.Bacc("TRN2", target_bir_lowering=False, num_devices=1)
    arrays, d = {}, _Dram()
    for pre, names in (("L0_attn_", _INS), ("L0_ffn_", _FFN_INS)):
        for name in names:
            a = _np.ascontiguousarray(inputs[pre + name])
            arrays[f"in_{name}_dram"] = a
            d.__dict__[name] = nc.dram_tensor(f"in_{name}_dram", a.shape, _mybir.dt.from_np(a.dtype),
                                              kind="ExternalInput").ap()
    d.out = nc.dram_tensor("out_dram", (B, T, D), F32, kind="ExternalOutput").ap()
    d.x1_dram = nc.dram_tensor("x1_dram", (B * T, D), F32).ap()
    for name in ("l_dram", "t_dram", "y_dram"):
        d.__dict__[name] = nc.dram_tensor(name, (2 * PER_HEAD * CH * SUBS * SUB, SUB), F32).ap()
    program(nc, d)
    r = _run(nc, [arrays], core_ids=[0])
    return r.results[0]["out_dram"]
```

```python
from contextlib import ExitStack

import concourse.bass as bass
from concourse import mybir

F32 = mybir.dt.float32
F32R = mybir.dt.float32r
U32 = mybir.dt.uint32
ALU = mybir.AluOpType
ACT = mybir.ActivationFunctionType
AX = mybir.AxisListType
LOG_EXP = "natural_log_exp_and_others"
SILU = "silu_and_others"
SILU_SET = "silu_and_others"

P = 128
B, T, D = 8, 256, 256
KT = D // P
H, DH = 16, 128
TAPS = 4
NE, RANK = 8, 128
LOW, INNER = 128, 1024
TILES = B * T // P
STEP = 4
STEPS = TILES // STEP
N = STEP * P
SUB = 32
SUBS = P // SUB
EPS = 1e-6
LN_EPS = 1e-5
FAR = -30720.0
G_HI, G_LO, BETA, CONV, TABLE = 0, TILES, 2 * TILES, 3 * TILES, 3 * TILES + 3 * TAPS


def wait(eng, sem, value):
    if isinstance(value, int) and value <= 0:
        return
    eng.wait_ge(sem, value)


def spread(ap, shape, axis=2):
    return ap.unsqueeze(axis).to_broadcast(shape)


class Semaphores:

    def __init__(self, nc, ctx, prefix):
        self.nc, self.prefix, self.all = nc, prefix, {}
        ctx.callback(self.release)

    def __call__(self, name):
        if name not in self.all:
            self.all[name] = self.nc.alloc_semaphore(name=self.prefix + name)
        return self.all[name]

    def release(self):
        self.nc.clear_and_free_semaphores(list(self.all.values()))
        self.nc.all_engine_barrier()



def ffn_buffers(nc, ctx, pre):
    def sb(name, shape, dt=F32):
        return ctx.enter_context(nc.sbuf_tensor(pre + name, shape, dt))

    class Buf:
        pass

    b = Buf()
    b.wa_raw = sb("wa_raw", [P, KT, NE * RANK])
    b.wa_hi = sb("wa_hi", [P, KT, NE * RANK], F32R)
    b.wa_lo = sb("wa_lo", [P, KT, NE * RANK], F32R)
    b.wb = sb("wb", [RANK, NE, D])
    b.router = sb("router", [P, KT, NE])
    b.sel_raw = sb("sel_raw", [2 * NE, NE, P])
    b.sel = sb("sel", [2 * NE, NE, P], F32R)
    b.iota = sb("iota", [P, NE])
    b.stats = sb("stats", [P, STEP, 6])
    b.mv = sb("mv", [P, STEP, 2])
    b.fence = sb("fence", [P, 2])
    b.lnv = sb("lnv", [P, STEP])
    b.rstd = sb("rstd", [P, STEP])
    b.q1 = sb("q1", [P, STEP])
    b.q2 = sb("q2", [P, STEP])
    b.q3 = sb("q3", [P, STEP])
    b.lnq = sb("lnq", [P, STEP])
    b.rn = sb("rn", [P, STEP])
    b.xn = sb("xn", [P, STEP, D])
    b.xnT = sb("xnT", [P, KT, N])
    b.xnT_hi = sb("xnT_hi", [P, KT, STEPS * N], F32R)
    b.xnT_lo = sb("xnT_lo", [P, KT, STEPS * N], F32R)
    b.logits = sb("logits", [P, STEP, NE])
    b.top = sb("top", [P, STEP, 8])
    b.topi = sb("topi", [P, STEP, 8], U32)
    b.topf = sb("topf", [P, STEP, 8])
    b.diff = sb("diff", [P, STEP, NE])
    b.diff2 = sb("diff2", [P, STEP, NE])
    b.ex = sb("ex", [P, STEP, NE])
    b.hit0 = sb("hit0", [P, STEP, NE])
    b.hit1 = sb("hit1", [P, STEP, NE])
    b.hits = sb("hits", [P, STEP, NE])
    b.chosen = sb("chosen", [P, STEP, NE])
    b.total = sb("total", [P, STEP])
    b.rtotal = sb("rtotal", [P, STEP])
    b.comb = sb("comb", [P, STEP, NE])
    b.comb2 = sb("comb2", [P, STEP, 2 * NE], F32R)
    b.combT = sb("combT", [2 * NE, STEPS * N], F32R)
    b.wide = [sb(f"wide{i}", [P, N]) for i in range(2)]
    b.hc = [sb(f"hc{i}", [P, N]) for i in range(2)]
    return b


def ffn_load(sp, b, S, router_w, Wa, Wb):
    sp.dma_start(b.wa_raw[:].rearrange("p k (e r) -> p k e r", e=NE)[:, 0],
                 Wa[:, 0:P, :].rearrange("e p r -> p e r")).then_inc(S("w_in"), 16)
    sp.dma_start(b.wa_raw[:].rearrange("p k (e r) -> p k e r", e=NE)[:, 1],
                 Wa[:, P:D, :].rearrange("e p r -> p e r")).then_inc(S("w_in"), 16)
    sp.dma_start(b.wb[:], Wb.rearrange("e r d -> r e d")).then_inc(S("wb_in"), 16)
    sp.dma_start(b.router[:], router_w.rearrange("(k p) e -> p k e", p=P)).then_inc(S("router_in"), 16)


def ffn_constants_pool(nc, pool, b, S):
    nc.gpsimd.memset(b.sel_raw[:], 0.0).then_inc(S("sel_made"), 1)
    pool.wait_ge(S("sel_made"), 1)
    for part in range(2):
        nc.gpsimd.affine_select(out=b.sel_raw[:], in_=b.sel_raw[:], compare_op=ALU.not_equal, fill=1.0,
                                base=-NE * part, pattern=[[-1, NE], [0, P]],
                                channel_multiplier=1).then_inc(S("sel_made"), 1)
        pool.wait_ge(S("sel_made"), 2 + part)
    nc.gpsimd.iota(b.iota[:], pattern=[[1, NE]], base=0, channel_multiplier=0,
                   allow_small_or_imprecise_dtypes=True).then_inc(S("iota_made"), 1)


def ffn_constants_vector(nc, dve, b, S):
    dve.wait_ge(S("sel_made"), 3)
    nc.vector.tensor_copy(b.sel[:], b.sel_raw[:]).then_inc(S("w_hi"), 1)
    dve.wait_ge(S("w_in"), 32)
    nc.vector.tensor_copy(b.wa_hi[:], b.wa_raw[:]).then_inc(S("w_hi"), 1)
    dve.wait_ge(S("w_hi"), 2)
    nc.vector.tensor_tensor(b.wa_lo[:], b.wa_raw[:], b.wa_hi[:].bitcast(F32),
                            ALU.subtract).then_inc(S("w_split"), 1)
    dve.wait_ge(S("iota_made"), 1)


def norm_stats_vector(nc, dve, b, S, n, src, tag, stats=None, mv=None):
    stats, mv = b.stats if stats is None else stats, b.mv if mv is None else mv
    for t in range(STEP):
        last = nc.vector.bn_stats(stats[:, t, :], src[:, t, :])
    last.then_inc(S(tag + "stats"), 1)
    dve.wait_ge(S(tag + "stats"), n + 1)
    nc.vector.memset(b.fence[:, 0:1], 0.0)
    for t in range(STEP):
        last = nc.vector.bn_aggr(mv[:, t, :], stats[:, t, :])
    last.then_inc(S(tag + "mv"), 1)


def columns(n):
    return slice(n * N, (n + 1) * N) if isinstance(n, int) else bass.ds(n * N, N)


def tiles(n):
    return slice(n * STEP, (n + 1) * STEP) if isinstance(n, int) else bass.ds(n * STEP, STEP)


def pair(n, i):
    return slice(n * STEP + 2 * i, n * STEP + 2 * i + 2) if isinstance(n, int) else bass.ds(n * STEP + 2 * i, 2)


def tile(n, t):
    return slice(n * STEP + t, n * STEP + t + 1) if isinstance(n, int) else bass.ds(n * STEP + t, 1)


def ffn_vector_normalise(nc, dve, b, S, n, x):
    dve.wait_ge(S("rstd"), n + 1)
    for t in range(STEP):
        last = nc.vector.tensor_scalar(b.xn[:, t, :], x[:, t, :], b.mv[:, t, 0:1], b.rstd[:, t:t + 1],
                                       ALU.subtract, ALU.mult)
    last.then_inc(S("xn"), 1)
    nc.vector.tensor_tensor(b.q1[:], b.mv[:, :, 1], b.rstd[:], ALU.mult).then_inc(S("q1"), 1)
    dve.wait_ge(S("q1"), n + 1)
    nc.vector.tensor_tensor(b.q2[:], b.q1[:], b.rstd[:], ALU.mult).then_inc(S("q2"), 1)
    dve.wait_ge(S("q2"), n + 1)
    nc.vector.tensor_scalar(b.q3[:], b.q2[:], float(D), 1e-24, ALU.mult, ALU.max).then_inc(S("q3"), 1)


def ffn_vector_split(nc, dve, b, S, n):
    dve.wait_ge(S("xnT"), n + 1)
    nc.vector.tensor_scalar(b.xnT_hi[:, :, columns(n)], b.xnT[:], 1.0, None, ALU.mult).then_inc(S("xnT_hi"), 1)
    dve.wait_ge(S("xnT_hi"), n + 1)
    nc.vector.tensor_tensor(b.xnT_lo[:, :, columns(n)], b.xnT[:], b.xnT_hi[:, :, columns(n)].bitcast(F32),
                            ALU.subtract).then_inc(S("xnT_lo"), 1)


def ffn_vector_select(nc, dve, b, S, n, bank):
    dve.wait_ge(S("router"), n + 1)
    nc.vector.tensor_copy(b.logits[:], bank[:, 0:STEP * NE].rearrange("p (t e) -> p t e", t=STEP)
                          ).then_inc(S("logits"), 1)
    dve.wait_ge(S("logits"), n + 1)
    nc.vector.memset(b.fence[:, 1:2], 0.0)
    for t in range(STEP):
        last = nc.vector.max(b.top[:, t, :], b.logits[:, t, :])
    last.then_inc(S("top"), 1)
    dve.wait_ge(S("top"), n + 1)
    nc.vector.tensor_tensor(b.diff[:], b.logits[:], b.top[:, :, 0:1].to_broadcast([P, STEP, NE]),
                            ALU.subtract).then_inc(S("diff"), 1)
    for t in range(STEP):
        last = nc.vector.max_index(b.topi[:, t, :], b.top[:, t, :], b.logits[:, t, :])
    last.then_inc(S("topi"), 1)
    dve.wait_ge(S("diff"), n + 1)
    dve.wait_ge(S("rn"), n + 1)
    nc.vector.tensor_tensor(b.diff2[:], b.diff[:], spread(b.rn[:, :], [P, STEP, NE]),
                            ALU.mult).then_inc(S("diff2"), 1)
    dve.wait_ge(S("topi"), n + 1)
    nc.vector.tensor_copy(b.topf[:], b.topi[:]).then_inc(S("topf"), 1)
    dve.wait_ge(S("topf"), n + 1)
    names = spread(b.iota[:, :], [P, STEP, NE], 1)
    nc.vector.tensor_tensor(b.hit0[:], names, b.topf[:, :, 0:1].to_broadcast([P, STEP, NE]), ALU.is_equal)
    nc.vector.tensor_tensor(b.hit1[:], names, b.topf[:, :, 1:2].to_broadcast([P, STEP, NE]),
                            ALU.is_equal).then_inc(S("hit"), 1)
    dve.wait_ge(S("hit"), n + 1)
    nc.vector.tensor_tensor(b.hits[:], b.hit0[:], b.hit1[:], ALU.add).then_inc(S("hits"), 1)


def ffn_vector_weigh(nc, dve, b, S, n):
    dve.wait_ge(S("hits"), n + 1)
    dve.wait_ge(S("ex"), n + 1)
    nc.vector.tensor_tensor(b.chosen[:], b.ex[:], b.hits[:], ALU.mult).then_inc(S("chosen"), 1)
    dve.wait_ge(S("chosen"), n + 1)
    nc.vector.tensor_reduce(b.total[:], b.chosen[:], AX.X, ALU.add).then_inc(S("total"), 1)
    dve.wait_ge(S("total"), n + 1)
    nc.vector.reciprocal(b.rtotal[:], b.total[:]).then_inc(S("rtotal"), 1)
    dve.wait_ge(S("rtotal"), n + 1)
    nc.vector.scalar_tensor_tensor(out=b.comb[:], in0=b.chosen[:], scalar=0.5,
                                   in1=spread(b.rtotal[:, :], [P, STEP, NE]),
                                   op0=ALU.mult, op1=ALU.mult).then_inc(S("comb"), 1)
    dve.wait_ge(S("comb"), n + 1)
    nc.vector.tensor_copy(b.comb2[:, :, 0:NE], b.comb[:]).then_inc(S("comb_hi"), 1)
    dve.wait_ge(S("comb_hi"), n + 1)
    nc.vector.tensor_tensor(b.comb2[:, :, NE:], b.comb[:], b.comb2[:, :, 0:NE].bitcast(F32),
                            ALU.subtract).then_inc(S("comb2"), 1)


def ffn_vector_weights_back(nc, dve, b, S, n, bank):
    dve.wait_ge(S("cT"), n + 1)
    nc.vector.tensor_scalar(b.combT[:, columns(n)], bank[0:2 * NE, :], 1.0, None, ALU.mult).then_inc(S("combT"), 1)


def ffn_vector_experts(nc, dve, b, S, n, bank_h, between):
    for e in range(NE):
        dve.wait_ge(S("wide"), n * NE + e + 1)
        if e >= 2:
            dve.wait_ge(S("down"), n * NE + e - 1)
        nc.vector.tensor_tensor(b.hc[e % 2][:], bank_h[e % 2][:], b.wide[e % 2][:],
                                ALU.mult).then_inc(S("hc"), 1)
        between(e)


def ffn_scalar_rstd(nc, act, b, S, n):
    act.wait_ge(S("f_mv"), n + 1)
    nc.scalar.activation(b.lnv[:], b.mv[:, :, 1], ACT.Ln, bias=LN_EPS).then_inc(S("lnv"), 1)
    act.wait_ge(S("lnv"), n + 1)
    nc.scalar.activation(b.rstd[:], b.lnv[:], ACT.Exp, scale=-0.5).then_inc(S("rstd"), 1)


def ffn_scalar_tokens(nc, act, b, S, n, bank_t):
    act.wait_ge(S("q3"), n + 1)
    nc.scalar.activation(b.lnq[:], b.q3[:], ACT.Ln, scale=float(2 ** 40)).then_inc(S("lnq"), 1)
    act.wait_ge(S("lnq"), n + 1)
    nc.scalar.activation(b.rn[:], b.lnq[:], ACT.Exp, scale=-0.5, bias=13.862943611198906).then_inc(S("rn"), 1)
    act.wait_ge(S("xT"), n + 1)
    for k in range(KT):
        last = nc.scalar.activation(b.xnT[:, k, :], bank_t[k][:], ACT.Copy)
    last.then_inc(S("xnT"), 1)


def ffn_scalar_exp(nc, act, b, S, n):
    act.wait_ge(S("diff2"), n + 1)
    nc.scalar.activation(b.ex[:], b.diff2[:], ACT.Exp).then_inc(S("ex"), 1)


def ffn_scalar_experts(nc, act, b, S, n, bank_c, between):
    for e in range(NE):
        act.wait_ge(S("up"), n * NE + e + 1)
        if e >= 2:
            act.wait_ge(S("hc"), n * NE + e - 1)
        nc.scalar.activation(b.wide[e % 2][:], bank_c[e % 2][:], ACT.Copy).then_inc(S("wide"), 1)
        between(e)


def ffn_tensor_turn(nc, pe, b, S, n, ident, bank_t):
    pe.wait_ge(S("xn"), n + 1)
    for k in range(KT):
        for t in range(STEP):
            last = nc.tensor.transpose(bank_t[k][:, t * P:(t + 1) * P], b.xn[:, t, k * P:(k + 1) * P], ident[:])
    last.then_inc(S("xT"), 1)


def ffn_tensor_router(nc, pe, b, S, n, bank):
    pe.wait_ge(S("xnT"), n + 1)
    for t in range(STEP):
        for k in range(KT):
            last = nc.tensor.matmul(bank[:, t * NE:(t + 1) * NE], b.xnT[:, k, t * P:(t + 1) * P],
                                    b.router[:, k, :], start=(k == 0), stop=(k == KT - 1))
    last.then_inc(S("router"), 1)


def ffn_tensor_weights(nc, pe, b, S, n, ident, bank):
    pe.wait_ge(S("comb2"), n + 1)
    for t in range(STEP):
        last = nc.tensor.transpose(bank[0:2 * NE, t * P:(t + 1) * P], b.comb2[:, t, :].bitcast(F32), ident[:])
    last.then_inc(S("cT"), 1)


def ffn_tensor_experts(nc, pe, b, S, n, bank_c, bank_h, bank_o, between):

    def up(e):
        cols = slice(e * RANK, (e + 1) * RANK)
        parts = [(w, x, k) for w, x in ((b.wa_hi, b.xnT_hi), (b.wa_hi, b.xnT_lo), (b.wa_lo, b.xnT_hi))
                 for k in range(KT)]
        for i, (w, x, k) in enumerate(parts):
            nc.tensor.matmul(bank_h[e % 2][:], w[:, k, cols], x[:, k, columns(n)], start=(i == 0),
                             stop=(i == len(parts) - 1))
        nc.tensor.matmul(bank_c[e % 2][:], b.sel[:, e, :], b.combT[:, columns(n)], start=True,
                         stop=True).then_inc(S("up"), 1)

    pe.wait_ge(S("combT"), n + 1)
    up(0)
    up(1)
    for e in range(NE):
        pe.wait_ge(S("hc"), n * NE + e + 1)
        for t in range(STEP):
            last = nc.tensor.matmul(bank_o[t // 2][:, (t % 2) * D:(t % 2 + 1) * D], b.hc[e % 2][:, t * P:(t + 1) * P],
                                    b.wb[:, e, :], start=(e == 0 and t % 2 == 0), stop=(e == NE - 1),
                                    skip_group_check=True)
        last.then_inc(S("down"), 1)
        if e + 2 < NE:
            up(e + 2)
        between(e)


def rounds_of_steps(eng, body):
    body(0)
    with eng.Fori(0, STEPS - 2) as i:
        body(i + 1)
    body(STEPS - 1)
    body(STEPS)





def persistent_buffers(nc, ctx):
    def sb(name, shape, dt=F32):
        return ctx.enter_context(nc.sbuf_tensor(name, shape, dt))

    class Buf:
        pass

    g = Buf()
    g.ident = sb("ident", [P, P])
    g.ident_r = sb("ident_r", [P, P], F32R)
    g.upto = sb("upto", [P, P])
    g.after_r = sb("after_r", [P, P], F32R)
    g.far_r = sb("far_r", [P, P], F32R)
    g.ones = sb("ones", [P, 1])
    g.ln1 = sb("ln1", [P, KT])
    g.ln2 = sb("ln2", [P, KT])
    g.onorm = sb("onorm", [P, 1])
    g.acc = sb("acc", [P, TILES, D])
    return g


def attention_buffers(nc, ctx, g):
    def sb(name, shape, dt=F32):
        return ctx.enter_context(nc.sbuf_tensor(name, shape, dt))

    g.hT_hi = sb("hT_hi", [P, KT, TILES * P], F32R)
    g.hT_lo = sb("hT_lo", [P, KT, TILES * P], F32R)
    g.gateT = sb("gateT", [LOW, TILES * P])
    g.table = sb("table", [P, H, TABLE])
    g.eg = sb("eg", [P, H, TILES])
    g.neg_eg = sb("neg_eg", [P, H, TILES])



def stage_one(nc, g, d):
    with ExitStack() as ctx:
        def sb(name, shape, dt=F32):
            return ctx.enter_context(nc.sbuf_tensor("s1_" + name, shape, dt))

        S = Semaphores(nc, ctx, "s1_")
        b = ffn_buffers(nc, ctx, "s1_")
        x_in = sb("x_in", [P, STEP, D])
        x1 = sb("x1", [P, STEP, D])
        hid = sb("hid", [P, STEP, D])
        hT = sb("hT", [P, KT, N])
        fa = sb("fa", [LOW, N])
        wfa = sb("wfa", [P, KT, LOW])
        wga = sb("wga", [P, KT, LOW])
        wfb = sb("wfb", [LOW, H])
        wbeta = sb("wbeta", [P, KT, H])
        a_log = sb("a_log", [P, H])
        ea = sb("ea", [P, H])
        dtb = sb("dtb", [P, H])
        mask = sb("mask", [P, 3, P])
        conv_rows = sb("conv_rows", [TAPS * H, 3, P])
        start = sb("start", [P, 1])
        stats2 = sb("stats2", [P, STEP, 6])
        mv2 = sb("mv2", [P, STEP, 2])
        lnv2 = sb("lnv2", [P, STEP])
        rstd2 = sb("rstd2", [P, STEP])
        v1 = sb("v1", [P, STEP])
        v2 = sb("v2", [P, STEP])
        lnr = sb("lnr", [P, STEP])
        rms = sb("rms", [P, STEP])
        both = sb("both", [P, STEP])
        z = sb("z", [P, STEP, H])
        zb = sb("zb", [P, STEP, H])
        az = sb("az", [P, STEP, H])
        ez = sb("ez", [P, STEP, H])
        lz = sb("lz", [P, STEP, H])
        ezb = sb("ezb", [P, STEP, H])
        sp_ = sb("softplus", [P, STEP, H])
        decay = sb("decay", [P, STEP, H])
        decay_hi = sb("decay_hi", [P, STEP, H], F32R)
        ezb1 = sb("ezb1", [P, STEP, H])
        beta = sb("beta", [P, STEP, H])

        bank = [ctx.enter_context(nc.psum_tensor(f"s1_bank{i}", [P, N], F32)) for i in range(8)]
        bank_t, bank_c, bank_h, bank_o = bank[0:2], bank[2:4], bank[4:6], bank[6:8]
        x_tiles = d.x.rearrange("b (c p) d -> p (b c) d", p=P)
        x1_tiles = d.x1_dram.rearrange("(n p) d -> p n d", p=P)

        def has_front(n):
            return not isinstance(n, int) or n < STEPS

        def has_experts(n):
            return not isinstance(n, int) or 0 < n <= STEPS

        def has_gates(n):
            return not isinstance(n, int) or n > 1

        def all_rounds(eng, body):
            for n in range(2):
                body(n)
            with eng.Fori(0, STEPS - 2) as i:
                body(i + 2)
            for n in range(STEPS, STEPS + 2):
                body(n)

        def each_piece(between):
            for e in range(NE):
                between(e)

        table_t = g.table[:].rearrange("p h f -> p f h")
        block = ctx.enter_context(nc.Block())

        @block.sync
        def _(sp):
            sp.dma_start(x_in[:], x_tiles[:, 0:STEP, :]).then_inc(S("x_in"), 16)
            sp.dma_start(g.acc[:], x_tiles).then_inc(S("x_all"), 16)
            ffn_load(sp, b, S, d.router_w, d.Wa, d.Wb)
            for dst, src in ((wfa, d.wfa), (wga, d.wga), (wbeta, d.wb)):
                sp.dma_start(dst[:], src.rearrange("(k p) n -> p k n", p=P)).then_inc(S("gates_in"), 16)
            sp.dma_start(wfb[:], d.wfb).then_inc(S("gates_in"), 16)
            for dst, src in ((a_log, d.a_log), (dtb, d.dt_bias)):
                sp.dma_start(dst[:], src.rearrange("(a h) -> a h", a=1).to_broadcast([P, H])).then_inc(S("gates_in"), 16)
            for dst, src in ((g.ln1, d.ln1_w), (g.ln2, d.ln2_w)):
                for k in range(KT):
                    sp.dma_start(dst[:, k:k + 1], src[k * P:(k + 1) * P].rearrange("(p a) -> p a", a=1)
                                 ).then_inc(S("gates_in"), 16)
            sp.dma_start(g.onorm[:], d.o_norm_w.rearrange("(p a) -> p a", a=1)).then_inc(S("gates_in"), 16)
            for c, src in enumerate((d.conv_q, d.conv_k, d.conv_v)):
                sp.dma_start(conv_rows[:, c, :], src.rearrange("t (h p) -> (t h) p", p=P)).then_inc(S("conv_in"), 16)
            def load(n):
                sp.wait_ge(S("xn"), n)
                sp.dma_start(x_in[:], x_tiles[:, tiles(n), :]).then_inc(S("x_in"), 16)

            def store(n):
                sp.wait_ge(S("x1"), n + 1)
                sp.dma_start(x1_tiles[:, tiles(n), :], x1[:]).then_inc(S("x1_out"), 16)

            load(1)
            with sp.Fori(0, STEPS - 2) as i:
                load(i + 2)
                store(i)
            store(STEPS - 2)
            store(STEPS - 1)
            sp.wait_ge(S("x1_out"), 16 * STEPS + 16)

        @block.gpsimd
        def _(pool):
            nc.gpsimd.memset(start[:], 0.0).then_inc(S("x1_out"), 16)
            nc.gpsimd.memset(g.ones[:], 1.0).then_inc(S("ones"), 1)
            nc.gpsimd.memset(g.ident[:], 0.0).then_inc(S("blank"), 1)
            nc.gpsimd.memset(g.upto[:], 1.0).then_inc(S("blank"), 1)
            nc.gpsimd.memset(mask[:, 0, :], 1.0).then_inc(S("blank"), 1)
            nc.gpsimd.memset(mask[:, 1, :], 0.0).then_inc(S("blank"), 1)
            pool.wait_ge(S("blank"), 4)
            nc.gpsimd.affine_select(out=g.ident[:], in_=g.ident[:], compare_op=ALU.not_equal, fill=1.0, base=0,
                                    pattern=[[-1, P]], channel_multiplier=1).then_inc(S("masks"), 1)
            nc.gpsimd.affine_select(out=g.upto[:], in_=g.upto[:], compare_op=ALU.is_ge, fill=0.0, base=0,
                                    pattern=[[1, P]], channel_multiplier=-1).then_inc(S("masks"), 1)
            nc.gpsimd.affine_select(out=mask[:, 0, :], in_=mask[:, 0, :], compare_op=ALU.is_ge, fill=0.0, base=-1,
                                    pattern=[[-1, P]], channel_multiplier=1).then_inc(S("masks"), 1)
            nc.gpsimd.affine_select(out=mask[:, 1, :], in_=mask[:, 1, :], compare_op=ALU.is_ge, fill=FAR, base=0,
                                    pattern=[[1, P]], channel_multiplier=-1).then_inc(S("masks"), 1)
            ffn_constants_pool(nc, pool, b, S)

        @block.vector
        def _(dve):
            dve.wait_ge(S("masks"), 4)
            nc.vector.tensor_copy(g.after_r[:], mask[:, 0, :])
            nc.vector.tensor_copy(g.far_r[:], mask[:, 1, :])
            nc.vector.tensor_copy(g.ident_r[:], g.ident[:]).then_inc(S("masks_r"), 1)
            ffn_constants_vector(nc, dve, b, S)
            dve.wait_ge(S("conv_T"), 1)
            for c in range(3):
                last = nc.vector.tensor_copy(
                    table_t[:, CONV + TAPS * c:CONV + TAPS * (c + 1), :],
                    bank[0][:, c * TAPS * H:(c + 1) * TAPS * H].rearrange("p (t h) -> p t h", t=TAPS))
            last.then_inc(S("conv"), 1)
            dve.wait_ge(S("conv"), 1)
            dve.wait_ge(S("gates_in"), 16 * 11)
            dve.wait_ge(S("ea"), 1)

            def attention_norms(n):
                dve.wait_ge(S("rstd2"), n + 1)
                nc.vector.tensor_tensor(v1[:], mv2[:, :, 1], rstd2[:], ALU.mult).then_inc(S("v1"), 1)
                for t in range(STEP):
                    nc.vector.tensor_scalar(g.acc[:, tile(n, t), :], x1[:, t:t + 1, :], mv2[:, t, 0:1],
                                            rstd2[:, t:t + 1], ALU.subtract, ALU.mult)
                dve.wait_ge(S("v1"), n + 1)
                nc.vector.tensor_tensor(v2[:], v1[:], rstd2[:], ALU.mult).then_inc(S("v2"), 1)
                dve.wait_ge(S("rms"), n + 1)
                nc.vector.tensor_tensor(both[:], rstd2[:], rms[:], ALU.mult).then_inc(S("both"), 1)
                dve.wait_ge(S("both"), n + 1)
                for t in range(STEP):
                    last = nc.vector.tensor_scalar(hid[:, t, :], x1[:, t, :], mv2[:, t, 0:1], both[:, t:t + 1],
                                                   ALU.subtract, ALU.mult)
                last.then_inc(S("hid"), 1)

            def attention_split(n):
                dve.wait_ge(S("hT"), n + 1)
                nc.vector.tensor_scalar(g.hT_hi[:, :, columns(n)], hT[:], 1.0, None, ALU.mult).then_inc(S("hT_hi"), 1)
                dve.wait_ge(S("hT_hi"), n + 1)
                nc.vector.tensor_tensor(g.hT_lo[:, :, columns(n)], hT[:], g.hT_hi[:, :, columns(n)].bitcast(F32),
                                        ALU.subtract)
                dve.wait_ge(S("low"), n + 1)
                nc.vector.tensor_scalar(g.gateT[:, columns(n)], bank_t[1][:], 1.0, None, ALU.mult)

            def gate_arguments(n):
                dve.wait_ge(S("gates"), n + 1)
                nc.vector.tensor_tensor(z[:], bank_t[0][:, 0:STEP * H].rearrange("p (t h) -> p t h", t=STEP),
                                        spread(dtb[:, :], [P, STEP, H], 1), ALU.add).then_inc(S("z"), 1)
                nc.vector.tensor_scalar(zb[:], bank_t[0][:, STEP * H:2 * STEP * H].rearrange("p (t h) -> p t h", t=STEP),
                                        -1.0, 80.0, ALU.mult, ALU.min).then_inc(S("zb"), 1)

            def gates(n):
                dve.wait_ge(S("lz"), n + 1)
                nc.vector.scalar_tensor_tensor(out=sp_[:], in0=z[:], scalar=0.0, in1=lz[:], op0=ALU.max,
                                               op1=ALU.add).then_inc(S("softplus"), 1)
                dve.wait_ge(S("softplus"), n + 1)
                nc.vector.scalar_tensor_tensor(out=decay[:], in0=sp_[:], scalar=-1.0,
                                               in1=spread(ea[:, :], [P, STEP, H], 1), op0=ALU.mult,
                                               op1=ALU.mult).then_inc(S("decay"), 1)
                dve.wait_ge(S("decay"), n + 1)
                nc.vector.tensor_copy(decay_hi[:], decay[:]).then_inc(S("decay_hi"), 1)
                dve.wait_ge(S("decay_hi"), n + 1)
                nc.vector.tensor_scalar(table_t[:, tiles(n), :], decay_hi[:].bitcast(F32), 1.0, None, ALU.mult)
                low = bass.ds(n * STEP + G_LO, STEP) if not isinstance(n, int) else slice(n * STEP + G_LO, (n + 1) * STEP + G_LO)
                nc.vector.tensor_tensor(table_t[:, low, :], decay[:], decay_hi[:].bitcast(F32), ALU.subtract)
                dve.wait_ge(S("ezb"), n + 1)
                nc.vector.tensor_scalar(ezb1[:], ezb[:], 1.0, None, ALU.add).then_inc(S("ezb1"), 1)
                dve.wait_ge(S("ezb1"), n + 1)
                nc.vector.reciprocal(beta[:], ezb1[:]).then_inc(S("beta"), 1)
                dve.wait_ge(S("beta"), n + 1)
                col = bass.ds(n * STEP + BETA, STEP) if not isinstance(n, int) else slice(n * STEP + BETA, (n + 1) * STEP + BETA)
                nc.vector.tensor_scalar(table_t[:, col, :], beta[:], 1.0, None, ALU.mult).then_inc(S("table"), 1)

            def body(n):
                def between(e):
                    if e == 0 and has_gates(n):
                        attention_norms(n - 2)
                    if e == 1 and has_front(n):
                        dve.wait_ge(S("x_in"), n * 16 + 16)
                        norm_stats_vector(nc, dve, b, S, n, x_in, "f_")
                    if e == 2 and has_gates(n):
                        attention_split(n - 2)
                    if e == 3:
                        if has_gates(n):
                            gate_arguments(n - 2)
                        if has_front(n):
                            ffn_vector_normalise(nc, dve, b, S, n, x_in)
                    if e == 4 and has_gates(n):
                        gates(n - 2)
                    if e == 5 and has_front(n):
                        ffn_vector_split(nc, dve, b, S, n)
                        ffn_vector_select(nc, dve, b, S, n, bank_t[0])
                    if e == 6 and has_front(n):
                        ffn_vector_weigh(nc, dve, b, S, n)
                    if e == 7 and has_front(n):
                        ffn_vector_weights_back(nc, dve, b, S, n, bank_t[1])

                if has_experts(n):
                    ffn_vector_experts(nc, dve, b, S, n - 1, bank_h, between)
                    if isinstance(n, int) and n == 1:
                        dve.wait_ge(S("x_all"), 16)
                    dve.wait_ge(S("down"), n * NE)
                    dve.wait_ge(S("x1_out"), n * 16)
                    for i in range(2):
                        last = nc.vector.tensor_tensor(
                            x1[:, 2 * i:2 * i + 2, :], bank_o[i][:].rearrange("p (t d) -> p t d", t=2),
                            g.acc[:, pair(n - 1, i), :], ALU.add)
                    last.then_inc(S("x1"), 1)
                    dve.wait_ge(S("x1"), n)
                    norm_stats_vector(nc, dve, b, S, n - 1, x1, "a_", stats2, mv2)
                else:
                    each_piece(between)

            all_rounds(dve, body)
            dve.wait_ge(S("eg"), 1)
            nc.vector.tensor_scalar(g.neg_eg[:], g.eg[:], -1.0, None, ALU.mult)

        @block.scalar
        def _(act):
            nc.scalar.preload_act_table_set(LOG_EXP)
            act.wait_ge(S("gates_in"), 16 * 11)
            nc.scalar.activation(ea[:], a_log[:], ACT.Exp).then_inc(S("ea"), 1)

            def attention_rms(n):
                act.wait_ge(S("a_mv"), n + 1)
                nc.scalar.activation(lnv2[:], mv2[:, :, 1], ACT.Ln, bias=LN_EPS).then_inc(S("lnv2"), 1)
                act.wait_ge(S("lnv2"), n + 1)
                nc.scalar.activation(rstd2[:], lnv2[:], ACT.Exp, scale=-0.5).then_inc(S("rstd2"), 1)
                act.wait_ge(S("v2"), n + 1)
                nc.scalar.activation(lnr[:], v2[:], ACT.Ln, bias=EPS).then_inc(S("lnr"), 1)
                act.wait_ge(S("lnr"), n + 1)
                nc.scalar.activation(rms[:], lnr[:], ACT.Exp, scale=-0.5).then_inc(S("rms"), 1)

            def attention_turned(n):
                act.wait_ge(S("hidT"), n + 1)
                for k in range(KT):
                    last = nc.scalar.activation(hT[:, k, :], bank_t[k][:], ACT.Copy, scale=g.ln1[:, k:k + 1])
                last.then_inc(S("hT"), 1)

            def gate_functions(n):
                act.wait_ge(S("z"), n + 1)
                nc.scalar.activation(az[:], z[:], ACT.Abs).then_inc(S("az"), 1)
                act.wait_ge(S("az"), n + 1)
                nc.scalar.activation(ez[:], az[:], ACT.Exp, scale=-1.0).then_inc(S("ez"), 1)
                act.wait_ge(S("ez"), n + 1)
                nc.scalar.activation(lz[:], ez[:], ACT.Ln, bias=1.0).then_inc(S("lz"), 1)
                act.wait_ge(S("zb"), n + 1)
                nc.scalar.activation(ezb[:], zb[:], ACT.Exp).then_inc(S("ezb"), 1)

            def body(n):
                def between(e):
                    if e == 0 and has_gates(n):
                        attention_rms(n - 2)
                    if e == 1 and has_gates(n):
                        attention_turned(n - 2)
                    if e == 2:
                        if has_front(n):
                            ffn_scalar_rstd(nc, act, b, S, n)
                        if has_gates(n):
                            act.wait_ge(S("low"), n - 1)
                            nc.scalar.activation(fa[:], bank_t[0][:], ACT.Copy).then_inc(S("fa"), 1)
                    if e == 3 and has_gates(n):
                        gate_functions(n - 2)
                    if e == 4 and has_front(n):
                        ffn_scalar_tokens(nc, act, b, S, n, bank_t)
                    if e == 6 and has_front(n):
                        ffn_scalar_exp(nc, act, b, S, n)

                if has_experts(n):
                    ffn_scalar_experts(nc, act, b, S, n - 1, bank_c, between)
                else:
                    each_piece(between)

            all_rounds(act, body)
            act.wait_ge(S("sums"), 1)
            nc.scalar.activation(g.eg[:], bank[0][:, 0:H * TILES].rearrange("p (h t) -> p h t", h=H),
                                 ACT.Exp).then_inc(S("eg"), 1)

        @block.tensor
        def _(pe):
            pe.wait_ge(S("masks"), 1)
            pe.wait_ge(S("conv_in"), 48)
            for c in range(3):
                last = nc.tensor.transpose(bank[0][:, c * TAPS * H:(c + 1) * TAPS * H], conv_rows[:, c, :],
                                           g.ident[0:TAPS * H, 0:TAPS * H])
            last.then_inc(S("conv_T"), 1)
            pe.wait_ge(S("conv"), 1)
            pe.wait_ge(S("gates_in"), 16 * 11)
            pe.wait_ge(S("wb_in"), 16)
            pe.wait_ge(S("router_in"), 16)

            def attention_turn(n):
                pe.wait_ge(S("hid"), n + 1)
                for k in range(KT):
                    for t in range(STEP):
                        last = nc.tensor.transpose(bank_t[k][:, t * P:(t + 1) * P], hid[:, t, k * P:(k + 1) * P],
                                                   g.ident[:])
                last.then_inc(S("hidT"), 1)

            def low_rank(n):
                pe.wait_ge(S("hT"), n + 1)
                for dst, w in ((bank_t[0], wfa), (bank_t[1], wga)):
                    for k in range(KT):
                        last = nc.tensor.matmul(dst[:], w[:, k, :], hT[:, k, :], start=(k == 0), stop=(k == KT - 1))
                last.then_inc(S("low"), 1)

            def gate_products(n):
                pe.wait_ge(S("fa"), n + 1)
                for t in range(STEP):
                    for k in range(KT):
                        nc.tensor.matmul(bank_t[0][:, (STEP + t) * H:(STEP + t + 1) * H], hT[:, k, t * P:(t + 1) * P],
                                         wbeta[:, k, :], start=(k == 0), stop=(k == KT - 1))
                for t in range(STEP):
                    last = nc.tensor.matmul(bank_t[0][:, t * H:(t + 1) * H], fa[:, t * P:(t + 1) * P], wfb[:],
                                            start=True, stop=True)
                last.then_inc(S("gates"), 1)

            def body(n):
                def between(e):
                    if e == 0 and has_gates(n):
                        attention_turn(n - 2)
                    if e == 1 and has_gates(n):
                        low_rank(n - 2)
                    if e == 2 and has_gates(n):
                        gate_products(n - 2)
                    if e == 3 and has_front(n):
                        ffn_tensor_turn(nc, pe, b, S, n, g.ident, bank_t)
                    if e == 4 and has_front(n):
                        ffn_tensor_router(nc, pe, b, S, n, bank_t[0])
                    if e == 6 and has_front(n):
                        ffn_tensor_weights(nc, pe, b, S, n, g.ident, bank_t[1])

                if has_experts(n):
                    ffn_tensor_experts(nc, pe, b, S, n - 1, bank_c, bank_h, bank_o, between)
                else:
                    each_piece(between)

            all_rounds(pe, body)
            pe.wait_ge(S("table"), STEPS)
            for i, part in enumerate((G_HI, G_LO)):
                last = nc.tensor.matmul(bank[0][:, 0:H * TILES], g.upto[:], g.table[:, :, part:part + TILES],
                                        start=(i == 0), stop=(i == 1))
            last.then_inc(S("sums"), 1)



CH = 4
UNITS = H * TILES // CH
PER_HEAD = TILES // CH
SLOTS = 2 * PER_HEAD
LEAD = SLOTS - 1
LOOPED = 6
BLOCKS = PER_HEAD * CH * SUBS


def stage_two(nc, g, d):
    with ExitStack() as ctx:
        def sb(name, shape, dt=F32):
            return ctx.enter_context(nc.sbuf_tensor("s2_" + name, shape, dt))

        S = Semaphores(nc, ctx, "s2_")
        Lt = [sb(f"Lt{s}", [P, CH, P]) for s in range(SLOTS)]
        QK = [sb(f"QK{s}", [P, CH, P]) for s in range(SLOTS)]
        Vn = [sb(f"Vn{s}", [P, CH, DH]) for s in range(SLOTS)]
        K1 = [sb(f"K1{s}", [P, 2, P]) for s in range(SLOTS)]
        Q1 = [sb(f"Q1{s}", [P, 2, P]) for s in range(SLOTS)]
        Kd = [sb(f"Kd{s}", [P, 2, DH]) for s in range(SLOTS)]
        cs = [sb(f"cs{s}", [P, 2 * CH]) for s in range(SLOTS)]
        w_raw = sb("w_raw", [P, 3, KT, DH])
        w_hi = [sb(f"w_hi{i}", [P, 3, KT, DH], F32R) for i in range(2)]
        w_lo = [sb(f"w_lo{i}", [P, 3, KT, DH], F32R) for i in range(2)]
        table = [sb(f"table{i}", [P, TABLE]) for i in range(2)]
        gm = [sb(f"gm_{p}", [P, CH, P], F32R) for p in ("hi", "lo")]
        conv = [sb(f"conv{i}", [P, N]) for i in range(3)]
        kT = sb("kT", [P, N])
        qT = sb("qT", [P, N])
        Pt_of = [sb(f"Pt{i}", [P, CH, P]) for i in range(2)]
        squares = sb("squares", [P, 2 * CH])
        ssq = sb("ssq", [P, CH])
        lnk = sb("lnk", [P, CH])
        nk = sb("nk", [P, CH])
        rk = sb("rk", [P, CH])
        blocks = sb("blocks", [2 * BLOCKS, SUB, SUB])
        Lb, eye = blocks[0:BLOCKS], blocks[BLOCKS:]
        Tb = sb("Tb", [BLOCKS, SUB, SUB])
        Yb = sb("Yb", [BLOCKS, SUB, SUB])
        outer = sb("outer", [BLOCKS, SUB * SUB // 4])
        Y = [sb(f"Y{i}", [P, CH, P]) for i in range(2)]
        TT = [sb(f"TT{i}", [P, CH, 2 * SUB]) for i in range(2)]
        F1 = sb("F1", [P, CH, SUB])
        F2 = sb("F2", [P, CH, 2 * SUB])
        U = sb("U", [P, CH, DH])
        St = sb("St", [P, 2, DH])
        QS = sb("QS", [P, CH, DH])
        O = sb("O", [P, CH, DH])
        OG = sb("OG", [P, N])
        gT = sb("gT", [P, N])
        junk = sb("junk", [P, CH, DH])
        so = sb("so", [P, CH])
        eo = sb("eo", [P, CH])
        lno = sb("lno", [P, CH])
        fo = sb("fo", [P, CH])
        eg = [sb(f"eg{i}", [P, 2, TILES]) for i in range(2)]
        wgb = [sb(f"wgb{i}", [LOW, DH]) for i in range(2)]
        wo = [sb(f"wo{i}", [P, D]) for i in range(2)]

        bank = [ctx.enter_context(nc.psum_tensor(f"s2_bank{i}", [P, N], F32)) for i in range(8)]
        bQ, bK, bV, bD, b4, b5, b6, b7 = bank

        def by_chunk(x):
            return x[:].rearrange("p (c i) -> p c i", c=CH)

        def half(ap, second):
            return ap.rearrange("p (b c) i -> p b c i", c=2)[:, :, second, :]

        def half_column(ap, second):
            return spread(ap.rearrange("p (b c) -> p b c", c=2)[:, :, second], [P, 2, DH])

        heads = [w.rearrange("(k p) (h n) -> p k h n", p=P, n=DH) for w in (d.wq, d.wk, d.wv)]
        wgb_h = d.wgb.rearrange("p (h n) -> p h n", n=DH)
        wo_h = d.wo.rearrange("(h p) n -> p h n", p=DH)
        shape = "(z u c s r) x -> z u c s r x"
        size = dict(z=2, u=PER_HEAD, c=CH, s=SUBS, r=SUB)
        Ld, Td, Yd = (x.rearrange(shape, **size) for x in (d.l_dram, d.t_dram, d.y_dram))
        flat = [x.rearrange("(z b r) x -> z b r x", z=2, r=SUB) for x in (d.l_dram, d.t_dram, d.y_dram)]

        class Round:

            def __init__(self, i, j):
                base = 0 if i is None else i * SLOTS
                self.m, self.n = base + j, base + (j + LEAD)
                self.hm, self.hn = (x // PER_HEAD if i is None else i * 2 + x // PER_HEAD for x in (j, j + LEAD))
                self.half_m = j // 2 if i is None else i * (SLOTS // 2) + j // 2
                self.um, self.un = j % PER_HEAD, (j + LEAD) % PER_HEAD
                self.pm, self.pn = (j // PER_HEAD) % 2, ((j + LEAD) // PER_HEAD) % 2
                self.sm, self.sn = j % SLOTS, (j + LEAD) % SLOTS
                self.y = j % 2
                self.ut, self.pt, self.st = (j - 1) % PER_HEAD, ((j - 1) // PER_HEAD) % 2, (j - 1) % SLOTS
                inside = i is not None
                self.front, self.back = inside or 0 <= self.n < UNITS, inside or 0 <= self.m < UNITS
                self.tail = inside or 1 <= self.m <= UNITS
                self.load = inside or 0 <= self.m + 1 < UNITS
                self.diag = inside or 1 <= self.n <= UNITS
                self.invert = self.un < PER_HEAD - 1 and (inside or 1 <= self.hn <= H)
                self.ready_back = self.um == PER_HEAD - 1 and (inside or 0 <= self.hm + 1 < H)
                self.ready_front = inside or 0 <= self.hn and self.hn + 1 < H

        def rounds(eng, body):
            for m in range(-LEAD, 1):
                body(Round(None, m))
            with eng.Fori(0, LOOPED) as i:
                for j in range(1, SLOTS + 1):
                    body(Round(i, j))
            for m in range(LOOPED * SLOTS + 1, UNITS + 1):
                body(Round(None, m))

        cuts = (0, 13, 25, SUB - 1)
        per_head = 2 * (SUB - 1)

        def at(h):
            return slice(h, h + 1) if isinstance(h, int) else bass.ds(h, 1)

        block = ctx.enter_context(nc.Block())

        @block.sync
        def _(sp):
            def load_front(h):
                for i, w in enumerate(heads):
                    sp.dma_start(w_raw[:, i], w[:, :, at(h), :]).then_inc(S("w_in"), 16)

            def load_back(h, p):
                sp.dma_start(wgb[p][:], wgb_h[:, at(h), :]).then_inc(S("wo_in"), 16)
                sp.dma_start(wo[p][:], wo_h[:, at(h), :]).then_inc(S("wo_in"), 16)

            load_front(0)
            load_back(0, 0)
            sp.wait_ge(S("w_split"), 1)
            load_front(1)
            sp.wait_ge(S("blank"), 1)
            sp.wait_ge(S("eye"), 2)
            sp.dma_start(Tb[:], eye).then_inc(S("lb_in"), 16)

            def body(r):
                more_front = r.un == 3 and (not isinstance(r.hn, int) or 0 <= r.hn and r.hn + 2 < H)
                more_back = r.um == 2 and (not isinstance(r.hm, int) or 0 <= r.hm and r.hm + 1 < H)
                if more_front and not r.diag:
                    sp.wait_ge(S("w_split"), r.hn + 2)
                if more_back and not r.diag:
                    sp.wait_ge(S("proj"), r.m - 1)
                if r.diag:
                    sp.wait_ge(S("Lt"), r.n)
                    slot, u, z = (r.sn - 1) % SLOTS, (r.un - 1) % PER_HEAD, r.pn if r.un else 1 - r.pn
                    for s in range(SUBS):
                        sub = slice(s * SUB, (s + 1) * SUB)
                        if s == 1 and more_front:
                            sp.wait_ge(S("w_split"), r.hn + 2)
                        if s == 2 and more_back:
                            sp.wait_ge(S("proj"), r.m - 1)
                        sp.dma_start(Ld[z, u, :, s].rearrange("c r x -> r c x"), Lt[slot][sub, :, sub]
                                     ).then_inc(S("l_out"), 16)
                    if r.un == 0:
                        sp.wait_ge(S("l_out"), r.n * (16 * SUBS))
                        sp.dma_start(Lb[:, 0:SUB // 4], flat[0][1 - r.pn][:, 0:SUB // 4]).then_inc(S("lb_in"), 16)
                        sp.dma_start(Lb[:, SUB // 4:], flat[0][1 - r.pn][:, SUB // 4:]).then_inc(S("lb_rest"), 16)
                if more_front:
                    load_front(r.hn + 2)
                if more_back:
                    load_back(r.hm + 1, 1 - r.pm)
                if r.invert and r.un == 2:
                    sp.wait_ge(S("inv"), r.hn * per_head)
                    unit = CH * SUBS
                    sp.dma_start(flat[1][1 - r.pn][0:unit], Tb[0:unit]).then_inc(S("t_out"), 16)
                    sp.wait_ge(S("inverted"), r.hn * 2)
                    sp.dma_start(flat[2][1 - r.pn][0:unit], Yb[0:unit]).then_inc(S("y_out"), 16)
                    if r.load:
                        wait(sp, S("W1"), r.m)
                    sp.dma_start(flat[1][1 - r.pn][unit:], Tb[unit:]).then_inc(S("others_out"), 16)
                    sp.dma_start(flat[2][1 - r.pn][unit:], Yb[unit:]).then_inc(S("others_out"), 16)
                    sp.wait_ge(S("t_out"), r.hn * 16)
                elif r.load:
                    wait(sp, S("W1"), r.m)
                if r.load:
                    u, z, y = (r.um + 1) % PER_HEAD, r.pm if r.um < 3 else 1 - r.pm, 1 - r.y
                    for s, (row, col) in enumerate(((0, 0), (SUB, SUB), (2 * SUB, 0))):
                        sp.dma_start(TT[y][row:row + SUB, :, col:col + SUB], Td[z, u, :, s].rearrange("c r x -> r c x")
                                     ).then_inc(S(f"tt_in{y}"), 16)
                if r.invert and r.un == 2:
                    sp.wait_ge(S("y_out"), r.hn * 16)
                if r.load:
                    for s in range(SUBS):
                        sub = slice(s * SUB, (s + 1) * SUB)
                        sp.dma_start(Y[y][sub, :, sub], Yd[z, u, :, s].rearrange("c r x -> r c x")
                                     ).then_inc(S(f"y_in{y}"), 16)
                if r.invert and r.un == 2:
                    sp.wait_ge(S("others_out"), r.hn * 32)
                if r.invert and r.un == 2 and (not isinstance(r.hn, int) or r.hn < H):
                    sp.dma_start(Tb[:], eye).then_inc(S("lb_in"), 16)

            rounds(sp, body)

        @block.gpsimd
        def _(pool):
            nc.gpsimd.memset(eye, 0.0).then_inc(S("eye"), 1)
            pool.wait_ge(S("eye"), 1)
            nc.gpsimd.affine_select(out=eye, in_=eye, compare_op=ALU.not_equal, fill=1.0, base=0,
                                    pattern=[[1, SUB], [-1, SUB]], channel_multiplier=0).then_inc(S("eye"), 1)
            pool.wait_ge(S("eye"), 2)

            def masked(u, p):
                nc.gpsimd.tensor_tensor(gm[0][:], spread(g.upto[:, :], [P, CH, P], 1),
                                        spread(table[p][:, G_HI + u * CH:G_HI + (u + 1) * CH], [P, CH, P]),
                                        ALU.mult).then_inc(S("gm_hi"), 1)

            pool.wait_ge(S("table"), 1)
            masked(0, 0)

            def body(r):
                if r.front and not (isinstance(r.n, int) and r.n + 1 == UNITS):
                    if r.un == 3:
                        pool.wait_ge(S("table"), r.hn + 2)
                    pool.wait_ge(S("D"), r.n + 1)
                    masked((r.un + 1) % PER_HEAD, r.pn if r.un < 3 else 1 - r.pn)
                if r.invert:
                    head = r.hn - 1
                    if r.un == 0:
                        pool.wait_ge(S("lb_in"), r.hn * 32)
                    for j in range(cuts[r.un], cuts[r.un + 1]):
                        if j == SUB // 4:
                            pool.wait_ge(S("lb_rest"), r.hn * 16)
                        shape = [BLOCKS, SUB - 1 - j, j + 1]
                        terms = outer[:, 0:shape[1] * shape[2]].rearrange("b (i x) -> b i x", i=shape[1])
                        if j > 0:
                            pool.wait_ge(S("inv"), head * per_head + 2 * j)
                        nc.gpsimd.tensor_tensor(terms, spread(Lb[:, j, j + 1:], shape), spread(Tb[:, j, 0:j + 1], shape, 1),
                                                ALU.mult).then_inc(S("inv"), 1)
                        pool.wait_ge(S("inv"), head * per_head + (2 * j + 1))
                        nc.gpsimd.tensor_tensor(Tb[:, j + 1:, 0:j + 1], Tb[:, j + 1:, 0:j + 1], terms,
                                                ALU.subtract).then_inc(S("inv"), 1)
                    if r.un == 2:
                        pool.wait_ge(S("inv"), head * per_head + per_head)
                        rows = slice(cuts[2] + 1, SUB)
                        shape = [BLOCKS, SUB, SUB - cuts[2] - 1]
                        nc.gpsimd.tensor_tensor(Yb[:, :, rows], Tb[:, rows, :].rearrange("b r c -> b c r"),
                                                spread(g.ones[0:BLOCKS, 0:1], shape), ALU.mult
                                                ).then_inc(S("inverted"), 1)

            rounds(pool, body)

        @block.vector
        def _(dve):
            def ready_table(h, p):
                nc.vector.tensor_scalar(table[p][:].unsqueeze(1), g.table[:, at(h), :], 1.0, None, ALU.mult
                                        ).then_inc(S("table"), 1)
                dve.wait_ge(S("w_in"), h * 48 + 48)
                nc.vector.tensor_copy(w_hi[p][:], w_raw[:]).then_inc(S("w_hi"), 1)

            def ready_lower(h, p):
                dve.wait_ge(S("w_hi"), h + 1)
                nc.vector.tensor_tensor(w_lo[p][:], w_raw[:], w_hi[p][:].bitcast(F32), ALU.subtract
                                        ).then_inc(S("w_split"), 1)

            def ready_back(h, p):
                for k, src in enumerate((g.eg, g.neg_eg)):
                    last = nc.vector.tensor_scalar(eg[p][:, k:k + 1, :], src[:, at(h), :], 1.0, None, ALU.mult)
                dve.wait_ge(S("wo_in"), h * 32 + 32)
                nc.vector.tensor_scalar(wo[p][:], wo[p][:], g.onorm[:, 0:1], None, ALU.mult
                                        ).then_inc(S("wo_ready"), 1)

            for x in (Y[0], Y[1], TT[0], TT[1], QS):
                last = nc.vector.memset(x[:], 0.0)
            last.then_inc(S("blank"), 1)
            nc.vector.memset(fo[:], 0.0).then_inc(S("acc"), 1)
            ready_table(0, 0)
            ready_lower(0, 0)

            def taps(r, c, ps, which):
                if which[0] == 1:
                    dve.wait_ge(S("tap"), r.n * 3 + (c + 1))
                for s in which:
                    out = conv[c][:].rearrange("p (b t) -> p b t", b=2)[:, :, s:]
                    if s > 1:
                        dve.wait_ge(S("taps"), r.n * 9 + (3 * c + s - 1))
                    nc.vector.scalar_tensor_tensor(
                        out=out, in0=ps[:].rearrange("p (b t) -> p b t", b=2)[:, :, 0:T - s],
                        scalar=table[r.pn][:, CONV + TAPS * c + 3 - s:CONV + TAPS * c + 4 - s],
                        in1=out, op0=ALU.mult, op1=ALU.add).then_inc(S("taps"), 1)

            def body(r):
                Pt = Pt_of[r.sn % 2]
                if r.front:
                    taps(r, 0, bQ, (1, 2, 3))
                if r.tail:
                    dve.wait_ge(S("KS"), r.m)
                    for c in (1, 3):
                        tile = r.ut * CH + c
                        last = nc.vector.scalar_tensor_tensor(
                            out=Vn[r.st][:, c, :], in0=b6[:, c * DH:(c + 1) * DH], scalar=eg[r.pt][:, 1, tile:tile + 1],
                            in1=Vn[r.st][:, c, :], op0=ALU.mult, op1=ALU.add)
                    last.then_inc(S("R1"), 1)
                if r.front:
                    taps(r, 1, bK, (1,))
                if r.tail:
                    dve.wait_ge(S("W1"), r.m)
                    nc.vector.tensor_tensor(half(U[:], 1), half(by_chunk(b5), 1), half_column(cs[r.st][:, 0:CH], 1),
                                            ALU.mult).then_inc(S("U1"), 1)
                if r.front:
                    taps(r, 1, bK, (2, 3))
                    taps(r, 2, bV, (1,))
                if r.tail:
                    dve.wait_ge(S("QSo"), r.m)
                    dve.wait_ge(S("Om"), r.m)
                    nc.vector.tensor_tensor(O[:], by_chunk(b6), QS[:], ALU.add).then_inc(S("O"), 1)
                if r.front:
                    taps(r, 2, bV, (2, 3))
                if r.back:
                    dve.wait_ge(S("W0"), r.m + 1)
                    nc.vector.tensor_tensor(half(U[:], 0), half(by_chunk(b5), 0), half_column(cs[r.sm][:, 0:CH], 0),
                                            ALU.mult).then_inc(S("U0"), 1)
                if r.tail:
                    dve.wait_ge(S("OT"), r.m)
                    dve.wait_ge(S("gT"), r.m)
                    nc.vector.tensor_tensor(OG[:], b7[:], gT[:], ALU.mult).then_inc(S("OG"), 1)
                if r.front:
                    dve.wait_ge(S("qk"), r.n + 1)
                    nc.vector.tensor_copy(K1[r.sn][:], half(by_chunk(kT), 1))
                    nc.vector.tensor_copy(Q1[r.sn][:], half(by_chunk(qT), 1))
                if r.tail:
                    dve.wait_ge(S("so"), r.m)
                    nc.vector.scalar_tensor_tensor(out=eo[:], in0=so[:], scalar=1.0 / DH,
                                                   in1=cs[r.st][:, CH:2 * CH], op0=ALU.mult,
                                                   op1=ALU.add).then_inc(S("eo"), 1)
                if r.front and r.ready_front and r.un == 0:
                    ready_table(r.hn + 1, 1 - r.pn)
                if r.front and r.ready_front and r.un == 1:
                    ready_lower(r.hn + 1, 1 - r.pn)
                if r.ready_back:
                    ready_back(r.hm + 1, 1 - r.pm)
                if r.front:
                    dve.wait_ge(S("k2"), r.n + 1)
                    nc.vector.tensor_scalar(ssq[:], squares[:, 0:CH], EPS, None, ALU.add).then_inc(S("norms"), 1)
                    nc.vector.tensor_tensor(Kd[r.sn][:], half(by_chunk(bD), 0),
                                            half(Pt[:], 0)[:, :, P - 1:P].to_broadcast([P, 2, DH]), ALU.mult
                                            ).then_inc(S("Kd"), 1)
                    dve.wait_ge(S("norms"), r.n + 1)
                    nc.vector.reciprocal(rk[:], ssq[:]).then_inc(S("rk"), 1)
                    dve.wait_ge(S("rk"), r.n + 1)
                    nc.vector.tensor_tensor(cs[r.sn][:, 0:CH], rk[:],
                                            table[r.pn][:, BETA + r.un * CH:BETA + (r.un + 1) * CH], ALU.mult
                                            ).then_inc(S("c"), 1)
                    dve.wait_ge(S("KK"), r.n + 1)
                    dve.wait_ge(S("c"), r.n + 1)
                    for c in range(CH):
                        last = nc.vector.scalar_tensor_tensor(
                            out=Lt[r.sn][:, c, :], in0=bQ[:, c * P:(c + 1) * P], scalar=cs[r.sn][:, c:c + 1],
                            in1=Pt[:, c, :], op0=ALU.mult, op1=ALU.mult)
                    last.then_inc(S("Lt"), 1)
                if r.tail:
                    dve.wait_ge(S("fo"), r.m)
                    dve.wait_ge(S("proj"), r.m)
                    for c in range(CH):
                        tile = g.acc[:, r.ut * CH + c, :]
                        ps = (b6, b7)[c // 2][:, (c % 2) * D:(c % 2 + 1) * D]
                        last = nc.vector.scalar_tensor_tensor(out=tile, in0=ps, scalar=fo[:, c:c + 1], in1=tile,
                                                              op0=ALU.mult, op1=ALU.add)
                    last.then_inc(S("acc"), 1)
                if r.front:
                    dve.wait_ge(S("KQ"), r.n + 1)
                    nc.vector.tensor_tensor(QK[r.sn][:], by_chunk(bK), Pt[:], ALU.mult).then_inc(S("QK"), 1)
                    dve.wait_ge(S("nk"), r.n + 1)
                    dve.wait_ge(S("vT"), r.n + 1)
                    nc.vector.tensor_tensor(Vn[r.sn][:], by_chunk(bV), spread(nk[:, :], [P, CH, DH]), ALU.mult
                                            ).then_inc(S("Vn"), 1)
                    dve.wait_ge(S("q2"), r.n + 1)
                    nc.vector.tensor_scalar(cs[r.sn][:, CH:2 * CH], squares[:, CH:2 * CH], EPS, float(DH) * EPS,
                                            ALU.add, ALU.mult).then_inc(S("epsilon"), 1)

            rounds(dve, body)

        @block.scalar
        def _(act):
            def tap(r, c, ps):
                act.wait_ge(S("qkv"), r.n * 3 + (c + 1))
                nc.scalar.activation(conv[c][:], ps[:], ACT.Copy,
                                     scale=table[r.pn][:, CONV + TAPS * c + 3:CONV + TAPS * c + 4]
                                     ).then_inc(S("tap"), 1)

            def masked(u, p):
                for c in range(CH):
                    col = G_LO + u * CH + c
                    last = nc.scalar.activation(gm[1][:, c, :], g.upto[:], ACT.Copy, scale=table[p][:, col:col + 1])
                last.then_inc(S("gm_lo"), 1)

            act.wait_ge(S("table"), 1)
            masked(0, 0)

            def body(r):
                Pt = Pt_of[r.sn % 2]
                if r.front:
                    act.wait_ge(S("D"), r.n + 1)
                    nc.scalar.activation(Pt[:], by_chunk(bD), ACT.Exp).then_inc(S("Pt"), 1)
                    if not (isinstance(r.n, int) and r.n + 1 == UNITS):
                        if r.un == 3:
                            act.wait_ge(S("table"), r.hn + 2)
                        masked((r.un + 1) % PER_HEAD, r.pn if r.un < 3 else 1 - r.pn)
                    if r.un == 0:
                        act.wait_ge(S("table"), r.hn + 1)
                    wait(act, S("q2"), r.n)
                    tap(r, 0, bQ)
                nc.scalar.preload_act_table_set(SILU)
                if r.tail:
                    act.wait_ge(S("QSm"), r.m)
                    for c in (1, 3):
                        tile = r.ut * CH + c
                        last = nc.scalar.activation(QS[:, c, :], b7[:, c * DH:(c + 1) * DH], ACT.Copy,
                                                    scale=eg[r.pt][:, 0, tile:tile + 1])
                    last.then_inc(S("QSo"), 1)
                if r.back:
                    act.wait_ge(S("F"), r.m + 1)
                    nc.scalar.activation(F1[SUB:2 * SUB], b4[SUB:2 * SUB, 0:CH * SUB].rearrange(
                        "p (c i) -> p c i", c=CH), ACT.Copy)
                    nc.scalar.activation(F1[3 * SUB:], b4[3 * SUB:, 0:CH * SUB].rearrange(
                        "p (c i) -> p c i", c=CH), ACT.Copy).then_inc(S("F1"), 1)
                if r.front:
                    tap(r, 1, bK)
                if r.back:
                    act.wait_ge(S("X"), r.m + 1)
                    for q in (0, 2):
                        nc.scalar.activation(Y[r.y][q * SUB:(q + 1) * SUB, :, (q + 1) * SUB:(q + 2) * SUB],
                                             b4[q * SUB:(q + 1) * SUB, 0:CH * SUB].rearrange("p (c i) -> p c i", c=CH),
                                             ACT.Copy, scale=-1.0)
                    nc.scalar.activation(TT[r.y][SUB:2 * SUB, :, 0:SUB],
                                         b4[SUB:2 * SUB, CH * SUB:2 * CH * SUB].rearrange("p (c i) -> p c i", c=CH),
                                         ACT.Copy, scale=-1.0).then_inc(S("merged"), 1)
                if r.back:
                    act.wait_ge(S("F'"), r.m + 1)
                    nc.scalar.activation(F2[2 * SUB:], b4[2 * SUB:, 0:CH * 2 * SUB].rearrange("p (c i) -> p c i", c=CH),
                                         ACT.Copy).then_inc(S("F2"), 1)
                if r.front:
                    tap(r, 2, bV)
                if r.front:
                    act.wait_ge(S("taps"), r.n * 9 + 3)
                    nc.scalar.activation(qT[:], conv[0][:], ACT.Silu)
                if r.invert and r.un == 2:
                    act.wait_ge(S("inv"), (r.hn - 1) * per_head + 2 * cuts[2])
                    rows = slice(0, cuts[2] + 1)
                    nc.scalar.activation(Yb[:, :, rows], Tb[:, rows, :].rearrange("b r c -> b c r"), ACT.Copy
                                         ).then_inc(S("inverted"), 1)
                if r.back:
                    act.wait_ge(S("X'"), r.m + 1)
                    nc.scalar.activation(Y[r.y][0:2 * SUB, :, 2 * SUB:], b4[0:2 * SUB, 0:CH * 2 * SUB].rearrange(
                        "p (c i) -> p c i", c=CH), ACT.Copy, scale=-1.0).then_inc(S("Y"), 1)
                if r.front:
                    act.wait_ge(S("taps"), r.n * 9 + 6)
                    nc.scalar.activation(kT[:], conv[1][:], ACT.Silu).then_inc(S("qk"), 1)
                if r.tail:
                    act.wait_ge(S("O"), r.m)
                    for c in range(CH):
                        last = nc.scalar.activation(junk[:, c, :], O[:, c, :], ACT.Square, accum_out=so[:, c:c + 1])
                    last.then_inc(S("so"), 1)
                if r.front:
                    act.wait_ge(S("taps"), r.n * 9 + 9)
                    nc.scalar.activation(conv[2][:], conv[2][:], ACT.Silu).then_inc(S("v"), 1)
                if r.back:
                    wait(act, S("OG"), r.m)
                    act.wait_ge(S("gate"), r.m + 1)
                    nc.scalar.activation(gT[:], bK[:], ACT.Silu).then_inc(S("gT"), 1)
                if r.front:
                    act.wait_ge(S("Kt"), r.n + 1)
                    for c in range(CH):
                        last = nc.scalar.activation(conv[1][:, c * P:(c + 1) * P], bD[:, c * P:(c + 1) * P], ACT.Square,
                                                    accum_out=squares[:, c:c + 1])
                    last.then_inc(S("k2"), 1)
                if r.back:
                    act.wait_ge(S("S"), r.m + 1)
                    nc.scalar.activation(St[:], half(by_chunk(b5), 1), ACT.Copy).then_inc(S("St"), 1)
                nc.scalar.preload_act_table_set(LOG_EXP)
                if r.front:
                    act.wait_ge(S("norms"), r.n + 1)
                    nc.scalar.activation(lnk[:], ssq[:], ACT.Ln).then_inc(S("lnk"), 1)
                if r.tail:
                    act.wait_ge(S("eo"), r.m)
                    nc.scalar.activation(lno[:], eo[:], ACT.Ln).then_inc(S("lno"), 1)
                if r.front:
                    act.wait_ge(S("lnk"), r.n + 1)
                    nc.scalar.activation(nk[:], lnk[:], ACT.Exp, scale=0.5).then_inc(S("nk"), 1)
                if r.tail:
                    act.wait_ge(S("lno"), r.m)
                    nc.scalar.activation(fo[:], lno[:], ACT.Exp, scale=-0.5).then_inc(S("fo"), 1)
                if r.front:
                    act.wait_ge(S("Qt"), r.n + 1)
                    for c in range(CH):
                        last = nc.scalar.activation(conv[0][:, c * P:(c + 1) * P], b4[:, c * P:(c + 1) * P], ACT.Square,
                                                    accum_out=squares[:, CH + c:CH + c + 1])
                    last.then_inc(S("q2"), 1)

            rounds(act, body)

        @block.tensor
        def _(pe):
            def project(r, c, ps, products=(0, 6), before_last=None):
                cols = slice(r.un * N, (r.un + 1) * N)
                parts = [(w, x, k) for w, x in ((w_hi, g.hT_hi), (w_hi, g.hT_lo), (w_lo, g.hT_hi)) for k in range(KT)]
                for i in range(*products):
                    if i == products[1] - 1 and before_last:
                        before_last()
                    w, x, k = parts[i]
                    last = nc.tensor.matmul(ps[:], w[r.pn][:, c, k, :], x[:, k, cols], start=(i == 0),
                                            stop=(i == len(parts) - 1), skip_group_check=True)
                if products[1] == len(parts):
                    last.then_inc(S("qkv"), 1)

            def body(r):
                tt_in = (S(f"tt_in{r.y}"), r.half_m * 48 + 48)
                y_in = (S(f"y_in{r.y}"), r.half_m * (16 * SUBS) + 16 * SUBS)
                up, low = slice(0, 2 * SUB), slice(2 * SUB, P)
                if r.front:
                    pe.wait_ge(S("gm_hi"), r.n + 1)
                    pe.wait_ge(S("gm_lo"), r.n + 1)
                    wait(pe, S("Kd"), r.n)
                    nc.tensor.matmul(bD[:], g.after_r[:], gm[0][:], start=True, stop=False)
                    nc.tensor.matmul(bD[:], g.after_r[:], gm[1][:], start=False, stop=False)
                    nc.tensor.matmul(bD[:], g.ident_r[:], spread(g.far_r[:, :], [P, CH, P], 1), start=False,
                                     stop=True).then_inc(S("D"), 1)
                    if r.un == 0:
                        pe.wait_ge(S("w_split"), r.hn + 1)
                    wait(pe, S("Lt"), r.n)
                    project(r, 0, bQ)
                if r.tail:
                    pe.wait_ge(S("acc"), r.m)
                    pe.wait_ge(S("St"), r.m)
                    for dst, x, sem in ((b6, K1, "KS"), (b7, Q1, "QSm")):
                        for i, c in enumerate((1, 3)):
                            last = nc.tensor.matmul(dst[:, c * DH:(c + 1) * DH], x[r.st][:, i, :], St[:, i, :],
                                                    start=True, stop=True)
                        last.then_inc(S(sem), 1)

                def merge_ready():
                    if r.back:
                        pe.wait_ge(*tt_in)
                        wait(pe, S("q2"), min(r.n, UNITS) if isinstance(r.n, int) else r.n)
                if r.front:
                    wait(pe, S("QK"), r.n)
                    project(r, 1, bK, before_last=merge_ready)
                else:
                    merge_ready()
                if r.back:
                    for c in range(CH):
                        for q in (0, 2):
                            rows, below = slice(q * SUB, (q + 1) * SUB), slice((q + 1) * SUB, (q + 2) * SUB)
                            last = nc.tensor.matmul(b4[below, c * SUB:(c + 1) * SUB], Lt[r.sm][rows, c, below],
                                                    TT[r.y][rows, c, 0:SUB], start=True, stop=True,
                                                    tile_position=(q * SUB, (q + 1) * SUB))
                    last.then_inc(S("F"), 1)

                def f1_ready():
                    if r.back:
                        pe.wait_ge(*y_in)
                        pe.wait_ge(S("F1"), r.m + 1)
                if r.front:
                    wait(pe, S("Vn"), r.n)
                    project(r, 2, bV, (0, 3), f1_ready)
                else:
                    f1_ready()
                if r.back:
                    for c in range(CH):
                        for q in (0, 2):
                            rows, below = slice(q * SUB, (q + 1) * SUB), slice((q + 1) * SUB, (q + 2) * SUB)
                            nc.tensor.matmul(b4[rows, c * SUB:(c + 1) * SUB], F1[below, c, :], Y[r.y][below, c, below],
                                             start=True, stop=True, tile_position=((q + 1) * SUB, q * SUB))
                        second = slice(SUB, 2 * SUB)
                        last = nc.tensor.matmul(b4[second, (CH + c) * SUB:(CH + c + 1) * SUB], Y[r.y][second, c, second],
                                                F1[second, c, :], start=True, stop=True, tile_position=(SUB, SUB))
                    last.then_inc(S("X"), 1)
                if r.tail:
                    pe.wait_ge(S("R1"), r.m)
                    for c in (1, 3):
                        last = nc.tensor.matmul(b5[:, c * DH:(c + 1) * DH], Y[1 - r.y][:, c, :], Vn[r.st][:, c, :],
                                                start=True, stop=True)
                    last.then_inc(S("W1"), 1)

                def blocks_ready():
                    if r.back:
                        pe.wait_ge(S("merged"), r.m + 1)
                if r.front:
                    project(r, 2, bV, (3, 6), blocks_ready)
                else:
                    blocks_ready()
                if r.back:
                    for c in range(CH):
                        last = nc.tensor.matmul(b4[low, c * 2 * SUB:(c + 1) * 2 * SUB], Lt[r.sm][up, c, low],
                                                TT[r.y][up, c, :], start=True, stop=True, tile_position=(0, 2 * SUB))
                    last.then_inc(S("F'"), 1)
                if r.tail:
                    pe.wait_ge(S("U1"), r.m)
                    for c in range(CH):
                        if c == CH - 1 and r.back:
                            pe.wait_ge(S("F2"), r.m + 1)
                        last = nc.tensor.matmul(b6[:, c * DH:(c + 1) * DH], QK[r.st][:, c, :], U[:, c, :],
                                                start=True, stop=True)
                    last.then_inc(S("Om"), 1)
                elif r.back:
                    pe.wait_ge(S("F2"), r.m + 1)
                if r.back:
                    for c in range(CH):
                        last = nc.tensor.matmul(b4[up, c * 2 * SUB:(c + 1) * 2 * SUB], F2[low, c, :],
                                                Y[r.y][low, c, low], start=True, stop=True, tile_position=(2 * SUB, 0))
                    last.then_inc(S("X'"), 1)
                    if r.um == 0:
                        pe.wait_ge(S("wo_ready"), r.hm + 1)
                    if r.front:
                        pe.wait_ge(S("taps"), r.n * 9 + 6)
                    nc.tensor.matmul(bK[:], wgb[r.pm][:], g.gateT[:, r.um * N:(r.um + 1) * N], start=True,
                                     stop=True).then_inc(S("gate"), 1)
                if r.tail:
                    pe.wait_ge(S("O"), r.m)
                    for c in range(CH):
                        last = nc.tensor.transpose(b7[:, c * P:(c + 1) * P], O[:, c, :], g.ident[:])
                    last.then_inc(S("OT"), 1)
                if r.back:
                    pe.wait_ge(S("Y"), r.m + 1)
                    for c in (0, 2):
                        last = nc.tensor.matmul(b5[:, c * DH:(c + 1) * DH], Y[r.y][:, c, :], Vn[r.sm][:, c, :],
                                                start=True, stop=True)
                    last.then_inc(S("W0"), 1)
                if r.front:
                    pe.wait_ge(S("qk"), r.n + 1)
                    for c in range(CH):
                        cols = slice(c * P, (c + 1) * P)
                        last = nc.tensor.matmul(bQ[:, cols], kT[:, cols], kT[:, cols], start=True, stop=True)
                    last.then_inc(S("KK"), 1)
                if r.front:
                    pe.wait_ge(S("Pt"), r.n + 1)
                    for ps, x, sem in ((bD, kT, "Kt"), (b4, qT, "Qt")):
                        for c in range(CH):
                            last = nc.tensor.transpose(ps[:, c * P:(c + 1) * P], x[:, c * P:(c + 1) * P], g.ident[:])
                        last.then_inc(S(sem), 1)
                if r.back:
                    pe.wait_ge(S("U0"), r.m + 1)
                    for i, c in enumerate((0, 2)):
                        last = nc.tensor.matmul(b5[:, (c + 1) * DH:(c + 2) * DH], Kd[r.sm][:, i, :], U[:, c, :],
                                                start=True, stop=True)
                    last.then_inc(S("S"), 1)
                if r.front:
                    if r.back:
                        pe.wait_ge(S("gT"), r.m + 1)
                    for c in range(CH):
                        cols = slice(c * P, (c + 1) * P)
                        last = nc.tensor.matmul(bK[:, cols], kT[:, cols], qT[:, cols], start=True, stop=True)
                    last.then_inc(S("KQ"), 1)
                    pe.wait_ge(S("v"), r.n + 1)
                    for c in range(CH):
                        last = nc.tensor.transpose(bV[:, c * P:(c + 1) * P], conv[2][:, c * P:(c + 1) * P], g.ident[:])
                    last.then_inc(S("vT"), 1)
                if r.tail:
                    pe.wait_ge(S("OG"), r.m)
                    for c in range(CH):
                        last = nc.tensor.matmul((b6, b7)[c // 2][:, (c % 2) * D:(c % 2 + 1) * D],
                                                OG[:, c * P:(c + 1) * P], wo[r.pt][:], start=True, stop=True)
                    last.then_inc(S("proj"), 1)

            rounds(pe, body)



def stage_three(nc, g, d):
    with ExitStack() as ctx:
        def sb(name, shape, dt=F32):
            return ctx.enter_context(nc.sbuf_tensor("s3_" + name, shape, dt))

        S = Semaphores(nc, ctx, "s3_")
        b = ffn_buffers(nc, ctx, "s3_")
        raw = sb("raw", [P, KT, INNER])
        w_gate = [sb(f"gate_{p}", [P, KT, INNER], F32R) for p in ("hi", "lo")]
        w_up = [sb(f"up_{p}", [P, KT, INNER], F32R) for p in ("hi", "lo")]
        w_down = sb("down", [P, INNER // P, D])
        x1 = sb("x1", [P, STEP, D])
        x2 = sb("x2", [P, STEP, D])
        out = sb("out", [P, STEP, D])
        h2 = sb("h2", [P, STEP, D])
        h2T = sb("h2T", [P, KT, N])
        start = sb("start", [P, 1])
        h2T_hi = sb("h2T_hi", [P, KT, N], F32R)
        h2T_lo = sb("h2T_lo", [P, KT, N], F32R)
        raw_gate = [raw[:, k, :] for k in range(KT)]
        raw_up = [x[:].rearrange("p t d -> p (t d)") for x in (out, b.xn)]
        squares = sb("squares", [P, STEP, D])
        ms = sb("ms", [P, STEP])
        lnm = sb("lnm", [P, STEP])
        rms = sb("rms", [P, STEP])
        act_g = [sb(f"act_g{i}", [P, N]) for i in range(2)]
        act_m = [sb(f"act_m{i}", [P, N]) for i in range(2)]

        bank = [ctx.enter_context(nc.psum_tensor(f"s3_bank{i}", [P, N], F32)) for i in range(8)]
        bank_t, bank_c, bank_h, bank_o = bank[0:2], bank[2:4], bank[4:6], bank[6:8]
        x1_tiles = d.x1_dram.rearrange("(n p) d -> p n d", p=P)
        out_tiles = d.out.rearrange("b (c p) d -> p (b c) d", p=P)
        NM = INNER // P

        def has_mlp(n):
            return not isinstance(n, int) or n < STEPS

        def has_experts(n):
            return not isinstance(n, int) or n > 0

        def has_next(n):
            return not isinstance(n, int) or n + 1 < STEPS

        def each_piece(between):
            for e in range(NE):
                between(e)

        block = ctx.enter_context(nc.Block())

        @block.sync
        def _(sp):
            sp.dma_start(x1[:], x1_tiles[:, 0:STEP, :]).then_inc(S("x1_in"), 16)
            for dst, src, name in ((raw_gate, d.w_gate, "gate"), (raw_up, d.w_up, "up")):
                for k in range(KT):
                    sp.dma_start(dst[k], src[k * P:(k + 1) * P, :]).then_inc(S(name + "_in"), 16)
            sp.dma_start(w_down[:], d.w_down.rearrange("(m p) n -> p m n", p=P)).then_inc(S("down_in"), 16)
            ffn_load(sp, b, S, d.router_w, d.Wa, d.Wb)
            sp.wait_ge(S("x12"), 1)
            sp.dma_start(x1[:], x1_tiles[:, STEP:2 * STEP, :]).then_inc(S("x1_in"), 16)
            with sp.Fori(0, STEPS - 2) as n:
                sp.wait_ge(S("x12"), n + 2)
                sp.dma_start(x1[:], x1_tiles[:, bass.ds(n * STEP + 2 * STEP, STEP), :]).then_inc(S("x1_in"), 16)
                sp.wait_ge(S("out"), n + 1)
                sp.dma_start(out_tiles[:, bass.ds(n * STEP, STEP), :], out[:]).then_inc(S("out_gone"), 16)
            for n in (STEPS - 2, STEPS - 1):
                sp.wait_ge(S("out"), n + 1)
                sp.dma_start(out_tiles[:, n * STEP:(n + 1) * STEP, :], out[:]).then_inc(S("out_gone"), 16)
            sp.wait_ge(S("out_gone"), 16 * STEPS + 16)

        @block.gpsimd
        def _(pool):
            nc.gpsimd.memset(start[:], 0.0).then_inc(S("out_gone"), 16)
            ffn_constants_pool(nc, pool, b, S)

        @block.vector
        def _(dve):
            def h2_front(n):
                dve.wait_ge(S("rms"), n + 1)
                for t in range(STEP):
                    last = nc.vector.tensor_scalar(h2[:, t:t + 1, :], g.acc[:, tile(n, t), :], rms[:, t:t + 1], None,
                                                   ALU.mult)
                last.then_inc(S("h2"), 1)

            def h2_split(n):
                dve.wait_ge(S("h2T"), n + 1)
                nc.vector.tensor_copy(h2T_hi[:], h2T[:]).then_inc(S("h2T_hi"), 1)
                dve.wait_ge(S("h2T_hi"), n + 1)
                nc.vector.tensor_tensor(h2T_lo[:], h2T[:], h2T_hi[:].bitcast(F32), ALU.subtract
                                        ).then_inc(S("h2T_lo"), 1)

            def body(n):
                if has_mlp(n):
                    for m in range(NM):
                        dve.wait_ge(S("silu"), n * NM + m + 1)
                        if m >= 2:
                            dve.wait_ge(S("mdown"), n * NM + m - 1)
                        nc.vector.tensor_tensor(act_m[m % 2][:], bank_c[m % 2][:], act_g[m % 2][:],
                                                ALU.mult).then_inc(S("act_m"), 1)
                    dve.wait_ge(S("x1_in"), n * 16 + 16)
                    nc.vector.tensor_tensor(x2[:], x1[:], g.acc[:, tiles(n), :], ALU.add).then_inc(S("x12"), 1)
                    dve.wait_ge(S("x12"), n + 1)
                    dve.wait_ge(S("mdown"), n * NM + NM)
                    for i in range(2):
                        last = nc.vector.tensor_tensor(x2[:, 2 * i:2 * i + 2, :], x2[:, 2 * i:2 * i + 2, :],
                                                       bank_o[i][:].rearrange("p (t d) -> p t d", t=2), ALU.add)
                    last.then_inc(S("x2"), 1)

                def between(e):
                    if e == 0 and has_mlp(n):
                        dve.wait_ge(S("x2"), n + 1)
                        norm_stats_vector(nc, dve, b, S, n, x2, "f_")
                    if e == 1:
                        if has_mlp(n):
                            nc.vector.tensor_scalar(g.acc[:, tiles(n), :], x2[:], 1.0, None, ALU.mult)
                        if has_next(n):
                            h2_front(n + 1)
                    if e == 2 and has_mlp(n):
                        ffn_vector_normalise(nc, dve, b, S, n, x2)
                    if e == 3 and has_next(n):
                        h2_split(n + 1)
                    if e == 4 and has_mlp(n):
                        ffn_vector_split(nc, dve, b, S, n)
                        ffn_vector_select(nc, dve, b, S, n, bank_t[0])
                    if e == 5 and has_mlp(n):
                        ffn_vector_weigh(nc, dve, b, S, n)
                    if e == 7 and has_mlp(n):
                        ffn_vector_weights_back(nc, dve, b, S, n, bank_t[1])

                if has_experts(n):
                    ffn_vector_experts(nc, dve, b, S, n - 1, bank_h, between)
                    dve.wait_ge(S("down"), n * NE)
                    dve.wait_ge(S("out_gone"), n * 16)
                    for i in range(2):
                        last = nc.vector.tensor_tensor(out[:, 2 * i:2 * i + 2, :], bank_o[i][:].rearrange("p (t d) -> p t d", t=2),
                                                       g.acc[:, pair(n - 1, i), :], ALU.add)
                    last.then_inc(S("out"), 1)
                else:
                    each_piece(between)

            h2_front(0)
            h2_split(0)
            for i, (w, x) in enumerate(((w_gate, raw_gate), (w_up, raw_up))):
                dve.wait_ge(S("mlp_hi"), i + 1)
                for k in range(KT):
                    last = nc.vector.tensor_tensor(w[1][:, k, :], x[k], w[0][:, k, :].bitcast(F32), ALU.subtract)
                last.then_inc(S("mlp_split"), 1)
            ffn_constants_vector(nc, dve, b, S)
            rounds_of_steps(dve, body)

        @block.scalar
        def _(act):
            def mean_square(n):
                for t in range(STEP):
                    last = nc.scalar.activation(squares[:, t:t + 1, :], g.acc[:, tile(n, t), :], ACT.Square,
                                                accum_out=ms[:, t:t + 1])
                last.then_inc(S("ms"), 1)
                act.wait_ge(S("ms"), n + 1)
                nc.scalar.activation(lnm[:], ms[:], ACT.Ln, scale=1.0 / D, bias=EPS).then_inc(S("lnm"), 1)
                act.wait_ge(S("lnm"), n + 1)
                nc.scalar.activation(rms[:], lnm[:], ACT.Exp, scale=-0.5).then_inc(S("rms"), 1)

            def turned(n):
                act.wait_ge(S("h2x"), n + 1)
                for k in range(KT):
                    last = nc.scalar.activation(h2T[:, k, :], bank_t[k][:], ACT.Copy, scale=g.ln2[:, k:k + 1])
                last.then_inc(S("h2T"), 1)

            def body(n):
                if has_mlp(n):
                    nc.scalar.preload_act_table_set(SILU)
                    for m in range(NM):
                        act.wait_ge(S("mup"), n * NM + m + 1)
                        if m >= 2:
                            act.wait_ge(S("act_m"), n * NM + m - 1)
                        nc.scalar.activation(act_g[m % 2][:], bank_h[m % 2][:], ACT.Silu
                                             ).then_inc(S("silu"), 1)
                    nc.scalar.preload_act_table_set(LOG_EXP)

                def between(e):
                    if e == 0 and has_next(n):
                        mean_square(n + 1)
                    if e == 1 and has_mlp(n):
                        ffn_scalar_rstd(nc, act, b, S, n)
                    if e == 2 and has_next(n):
                        turned(n + 1)
                    if e == 3 and has_mlp(n):
                        ffn_scalar_tokens(nc, act, b, S, n, bank_t)
                    if e == 5 and has_mlp(n):
                        ffn_scalar_exp(nc, act, b, S, n)

                if has_experts(n):
                    ffn_scalar_experts(nc, act, b, S, n - 1, bank_c, between)
                else:
                    each_piece(between)

            nc.scalar.preload_act_table_set(LOG_EXP)
            mean_square(0)
            turned(0)
            for w, x, name in ((w_gate, raw_gate, "gate"), (w_up, raw_up, "up")):
                act.wait_ge(S(name + "_in"), 32)
                for k in range(KT):
                    last = nc.scalar.activation(w[0][:, k, :], x[k], ACT.Copy)
                last.then_inc(S("mlp_hi"), 1)
            rounds_of_steps(act, body)

        @block.tensor
        def _(pe):
            def turn(n):
                pe.wait_ge(S("h2"), n + 1)
                for k in range(KT):
                    for t in range(STEP):
                        last = nc.tensor.transpose(bank_t[k][:, t * P:(t + 1) * P], h2[:, t, k * P:(k + 1) * P], g.ident[:])
                last.then_inc(S("h2x"), 1)

            def up(m):
                cols = slice(m * P, (m + 1) * P)
                for dst, w in ((bank_h[m % 2], w_gate), (bank_c[m % 2], w_up)):
                    parts = [(u, x, k) for u, x in ((w[0], h2T_hi), (w[0], h2T_lo), (w[1], h2T_hi))
                             for k in range(KT)]
                    for i, (u, x, k) in enumerate(parts):
                        last = nc.tensor.matmul(dst[:], u[:, k, cols], x[:, k, :], start=(i == 0),
                                                stop=(i == len(parts) - 1))
                last.then_inc(S("mup"), 1)

            def body(n):
                if has_mlp(n):
                    pe.wait_ge(S("h2T_lo"), n + 1)
                    up(0)
                    up(1)
                    for m in range(NM):
                        pe.wait_ge(S("act_m"), n * NM + m + 1)
                        for t in range(STEP):
                            last = nc.tensor.matmul(bank_o[t // 2][:, (t % 2) * D:(t % 2 + 1) * D],
                                                    act_m[m % 2][:, t * P:(t + 1) * P], w_down[:, m, :],
                                                    start=(m == 0 and t % 2 == 0), stop=(m == NM - 1),
                                                    skip_group_check=True)
                        last.then_inc(S("mdown"), 1)
                        if m + 2 < NM:
                            up(m + 2)

                def between(e):
                    if e == 1 and has_next(n):
                        turn(n + 1)
                    if e == 3 and has_mlp(n):
                        if has_next(n):
                            pe.wait_ge(S("h2T"), n + 2)
                        ffn_tensor_turn(nc, pe, b, S, n, g.ident, bank_t)
                    if e == 4 and has_mlp(n):
                        ffn_tensor_router(nc, pe, b, S, n, bank_t[0])
                    if e == 6 and has_mlp(n):
                        ffn_tensor_weights(nc, pe, b, S, n, g.ident, bank_t[1])

                if has_experts(n):
                    ffn_tensor_experts(nc, pe, b, S, n - 1, bank_c, bank_h, bank_o, between)
                else:
                    each_piece(between)

            turn(0)
            pe.wait_ge(S("mlp_split"), 2)
            pe.wait_ge(S("down_in"), 16)
            pe.wait_ge(S("wb_in"), 16)
            pe.wait_ge(S("router_in"), 16)
            rounds_of_steps(pe, body)


def program(nc, d):
    with ExitStack() as ctx:
        g = persistent_buffers(nc, ctx)
        with ExitStack() as attention:
            attention_buffers(nc, attention, g)
            stage_one(nc, g, d)
            stage_two(nc, g, d)
        stage_three(nc, g, d)


_INS = ['x', 'wq', 'wk', 'wv', 'conv_q', 'conv_k', 'conv_v', 'wfa', 'wfb', 'wb', 'wga', 'wgb', 'a_log', 'dt_bias',
        'o_norm_w', 'wo', 'ln1_w', 'ln2_w', 'w_gate', 'w_up', 'w_down']
_FFN_INS = ['router_w', 'Wa', 'Wb']


class _Dram:
    pass


def kernel(**inputs):
    import numpy as _np
    import concourse.bacc as _bacc
    from concourse import mybir as _mybir
    from concourse.bass_utils import run_bass_kernel_spmd as _run

    nc = _bacc.Bacc("TRN2", target_bir_lowering=False, num_devices=1)
    arrays, d = {}, _Dram()
    for pre, names in (("L0_attn_", _INS), ("L0_ffn_", _FFN_INS)):
        for name in names:
            a = _np.ascontiguousarray(inputs[pre + name])
            arrays[f"in_{name}_dram"] = a
            d.__dict__[name] = nc.dram_tensor(f"in_{name}_dram", a.shape, _mybir.dt.from_np(a.dtype),
                                              kind="ExternalInput").ap()
    d.out = nc.dram_tensor("out_dram", (B, T, D), F32, kind="ExternalOutput").ap()
    d.x1_dram = nc.dram_tensor("x1_dram", (B * T, D), F32).ap()
    for name in ("l_dram", "t_dram", "y_dram"):
        d.__dict__[name] = nc.dram_tensor(name, (2 * PER_HEAD * CH * SUBS * SUB, SUB), F32).ap()
    program(nc, d)
    r = _run(nc, [arrays], core_ids=[0])
    return r.results[0]["out_dram"]
```
